# Optimizing a Trainium2 kernel written in Bass

```python
import numpy as np
import jax
import jax.numpy as jnp

def _softmax(x, axis=-1):
    return jax.nn.softmax(x, axis=axis)

def _gelu(x):
    return jax.nn.gelu(x, approximate=True)

def _silu(x):
    return jax.nn.silu(x)

def _sigmoid(x):
    return jax.nn.sigmoid(x)

def _layernorm(x, axis=-1, eps=1e-05):
    m = jnp.mean(x, axis=axis, keepdims=True)
    v = jnp.var(x, axis=axis, keepdims=True)
    return (x - m) / jnp.sqrt(v + eps)

def _scatter_add(tgt, idx, src, axis=0):
    return tgt.at[idx].add(src)

def _segment_sum(src, seg, n):
    return jax.ops.segment_sum(src, seg, n)
kernel_name = 'mk_adaln_d2_jaxref_r8_4f0694'

def setup_inputs(seed: int=0):
    np.random.seed(seed)
    _w = jnp.asarray

    def _L0_attn_setup():
        import jax, jax.numpy as jnp
        import numpy as np
        B, T, D = (4, 512, 128)
        F = 4 * D
        EPS_INIT = -1e+30

        def layer_norm(x, w, b, eps=1e-05):
            mu = jnp.mean(x, axis=-1, keepdims=True)
            var = jnp.var(x, axis=-1, keepdims=True)
            return (x - mu) * jax.lax.rsqrt(var + eps) * w + b

        def time_shift(x):
            return jnp.concatenate([jnp.zeros_like(x[:, :1]), x[:, :-1]], axis=1)

        def wkv(w, u, k, v):
            bsz, _, dim = k.shape
            alpha0 = jnp.zeros((bsz, dim), k.dtype)
            beta0 = jnp.zeros((bsz, dim), k.dtype)
            eps0 = jnp.full((bsz, dim), EPS_INIT, k.dtype)

            def step(carry, kv_t):
                alpha, beta, eps = carry
                kt, vt = kv_t
                ukt = u + kt
                tau = jnp.maximum(ukt, eps)
                e1 = jnp.exp(eps - tau)
                e2 = jnp.exp(ukt - tau)
                out = (e1 * alpha + e2 * vt) / (e1 * beta + e2)
                weps = eps - w
                tau2 = jnp.maximum(weps, kt)
                d1 = jnp.exp(weps - tau2)
                d2 = jnp.exp(kt - tau2)
                return ((d1 * alpha + d2 * vt, d1 * beta + d2, tau2), out)
            kT = jnp.swapaxes(k, 0, 1)
            vT = jnp.swapaxes(v, 0, 1)
            _, outT = jax.lax.scan(step, (alpha0, beta0, eps0), (kT, vT))
            return jnp.swapaxes(outT, 0, 1)
        key = jax.random.key(seed)
        ks = jax.random.split(key, 20)
        n = lambda k, shape, s: jax.random.normal(k, shape, jnp.float32) * s
        u = lambda k, shape: jax.random.uniform(k, shape, jnp.float32)
        s = 0.02
        return {'x': jax.random.normal(ks[0], (B, T, D), jnp.float32), 'ln1_w': jnp.ones((D,), jnp.float32), 'ln1_b': jnp.zeros((D,), jnp.float32), 'ln2_w': jnp.ones((D,), jnp.float32), 'ln2_b': jnp.zeros((D,), jnp.float32), 'time_decay': n(ks[1], (D,), 0.5), 'time_first': n(ks[2], (D,), 0.5), 'time_mix_k': u(ks[3], (1, 1, D)), 'time_mix_v': u(ks[4], (1, 1, D)), 'time_mix_r': u(ks[5], (1, 1, D)), 'w_key': n(ks[6], (D, D), s), 'w_value': n(ks[7], (D, D), s), 'w_recept': n(ks[8], (D, D), s), 'w_output': n(ks[9], (D, D), s), 'f_time_mix_k': u(ks[10], (1, 1, D)), 'f_time_mix_r': u(ks[11], (1, 1, D)), 'f_w_key': n(ks[12], (D, F), s), 'f_w_recept': n(ks[13], (D, D), s), 'f_w_value': n(ks[14], (F, D), s)}
    _L0_attn_in = _L0_attn_setup()

    def _L0_ffn_setup():
        import jax, jax.numpy as jnp
        import numpy as np
        HIDDEN = 128
        INTER = 512
        key = jax.random.key(seed)
        k1, k2, k3, k4, k5 = jax.random.split(key, 5)
        hidden_states = jax.random.normal(k1, (4, 256, HIDDEN), dtype=jnp.float32)
        W1 = jax.random.normal(k2, (HIDDEN, INTER), dtype=jnp.float32) * (1.0 / np.sqrt(HIDDEN))
        b1 = jax.random.normal(k3, (INTER,), dtype=jnp.float32) * 0.02
        W2 = jax.random.normal(k4, (INTER, HIDDEN), dtype=jnp.float32) * (1.0 / np.sqrt(INTER))
        b2 = jax.random.normal(k5, (HIDDEN,), dtype=jnp.float32) * 0.02
        return {'hidden_states': hidden_states, 'W1': W1, 'b1': b1, 'W2': W2, 'b2': b2}
    _L0_ffn_in = _L0_ffn_setup()
    _L0_c = _w((lambda *s: np.random.randn(*s).astype(np.float32) * 0.05)(32, 128))
    _L0_wmod = _w((lambda *s: np.random.randn(*s).astype(np.float32) * 0.05)(128, 6 * 128) * 128 ** (-0.5))

    def _L1_attn_setup():
        import jax, jax.numpy as jnp
        import numpy as np
        DIM, H, G = (128, 16, 4)
        HD = DIM // H
        HKV = H // G

        def rotate_half(x):
            return jnp.concatenate([-x[..., 1::2], x[..., ::2]], axis=-1)

        def rope_tables(seq_len, dim, dtype):
            inv_freq = 1.0 / 10000.0 ** (jnp.arange(0, dim, 2, dtype=jnp.float32) / dim)
            pos = jnp.arange(seq_len, dtype=jnp.float32)
            sinusoid = pos[:, None] * inv_freq[None, :]
            sin = jnp.concatenate([jnp.sin(sinusoid)] * 2, -1)
            cos = jnp.concatenate([jnp.cos(sinusoid)] * 2, -1)
            return (sin.astype(dtype)[None, :, None, :], cos.astype(dtype)[None, :, None, :])
        key = jax.random.key(seed)
        ks = jax.random.split(key, 9)
        s = 0.02
        return {'hidden_states': jax.random.normal(ks[0], (2, 256, DIM), jnp.float32), 'Wq': jax.random.normal(ks[1], (DIM, DIM), jnp.float32) * s, 'bq': jnp.zeros((DIM,), jnp.float32), 'Wk': jax.random.normal(ks[2], (DIM // G, DIM), jnp.float32) * s, 'bk': jnp.zeros((DIM // G,), jnp.float32), 'Wv': jax.random.normal(ks[3], (DIM // G, DIM), jnp.float32) * s, 'bv': jnp.zeros((DIM // G,), jnp.float32), 'Wo': jax.random.normal(ks[4], (DIM, DIM), jnp.float32) * s, 'bo': jnp.zeros((DIM,), jnp.float32)}
    _L1_attn_in = _L1_attn_setup()

    def _L1_ffn_setup():
        import jax, jax.numpy as jnp
        import numpy as np
        N_EMBD = 128
        NUM_EXPERTS = 8
        TOP_K = 2
        D_FF = 4 * N_EMBD
        B, S = (4, 256)
        key = jax.random.key(seed)
        ks = jax.random.split(key, 7)
        scale = lambda fan_in: 1.0 / np.sqrt(fan_in)
        x = jax.random.normal(ks[0], (B, S, N_EMBD), dtype=jnp.float32)
        W_router = jax.random.normal(ks[1], (N_EMBD, NUM_EXPERTS), dtype=jnp.float32) * scale(N_EMBD)
        b_router = jnp.zeros((NUM_EXPERTS,), dtype=jnp.float32)
        W1 = jax.random.normal(ks[2], (NUM_EXPERTS, N_EMBD, D_FF), dtype=jnp.float32) * scale(N_EMBD)
        b1 = jnp.zeros((NUM_EXPERTS, D_FF), dtype=jnp.float32)
        W2 = jax.random.normal(ks[3], (NUM_EXPERTS, D_FF, N_EMBD), dtype=jnp.float32) * scale(D_FF)
        b2 = jnpp = jnp.zeros((NUM_EXPERTS, N_EMBD), dtype=jnp.float32)
        return {'x': x, 'W_router': W_router, 'b_router': b_router, 'W1': W1, 'b1': b1, 'W2': W2, 'b2': b2}
    _L1_ffn_in = _L1_ffn_setup()
    _L1_c = _w((lambda *s: np.random.randn(*s).astype(np.float32) * 0.05)(32, 128))
    _L1_wmod = _w((lambda *s: np.random.randn(*s).astype(np.float32) * 0.05)(128, 6 * 128) * 128 ** (-0.5))
    _d = {'L0_attn_x': _L0_attn_in['x'], 'L0_attn_ln1_w': _L0_attn_in['ln1_w'], 'L0_attn_ln1_b': _L0_attn_in['ln1_b'], 'L0_attn_ln2_w': _L0_attn_in['ln2_w'], 'L0_attn_ln2_b': _L0_attn_in['ln2_b'], 'L0_attn_time_decay': _L0_attn_in['time_decay'], 'L0_attn_time_first': _L0_attn_in['time_first'], 'L0_attn_time_mix_k': _L0_attn_in['time_mix_k'], 'L0_attn_time_mix_v': _L0_attn_in['time_mix_v'], 'L0_attn_time_mix_r': _L0_attn_in['time_mix_r'], 'L0_attn_w_key': _L0_attn_in['w_key'], 'L0_attn_w_value': _L0_attn_in['w_value'], 'L0_attn_w_recept': _L0_attn_in['w_recept'], 'L0_attn_w_output': _L0_attn_in['w_output'], 'L0_attn_f_time_mix_k': _L0_attn_in['f_time_mix_k'], 'L0_attn_f_time_mix_r': _L0_attn_in['f_time_mix_r'], 'L0_attn_f_w_key': _L0_attn_in['f_w_key'], 'L0_attn_f_w_recept': _L0_attn_in['f_w_recept'], 'L0_attn_f_w_value': _L0_attn_in['f_w_value'], 'L0_ffn_W1': _L0_ffn_in['W1'], 'L0_ffn_b1': _L0_ffn_in['b1'], 'L0_ffn_W2': _L0_ffn_in['W2'], 'L0_ffn_b2': _L0_ffn_in['b2'], 'L0_c': _L0_c, 'L0_wmod': _L0_wmod, 'L1_attn_Wq': _L1_attn_in['Wq'], 'L1_attn_bq': _L1_attn_in['bq'], 'L1_attn_Wk': _L1_attn_in['Wk'], 'L1_attn_bk': _L1_attn_in['bk'], 'L1_attn_Wv': _L1_attn_in['Wv'], 'L1_attn_bv': _L1_attn_in['bv'], 'L1_attn_Wo': _L1_attn_in['Wo'], 'L1_attn_bo': _L1_attn_in['bo'], 'L1_ffn_W_router': _L1_ffn_in['W_router'], 'L1_ffn_b_router': _L1_ffn_in['b_router'], 'L1_ffn_W1': _L1_ffn_in['W1'], 'L1_ffn_b1': _L1_ffn_in['b1'], 'L1_ffn_W2': _L1_ffn_in['W2'], 'L1_ffn_b2': _L1_ffn_in['b2'], 'L1_c': _L1_c, 'L1_wmod': _L1_wmod}
    _x0 = _d['L0_attn_x']
    _d['L0_attn_x'] = jax.random.normal(jax.random.fold_in(jax.random.key(seed), 1), (32, 256, 128), dtype=_x0.dtype)
    del _x0
    return _d

def reference(L0_attn_x, L0_attn_ln1_w, L0_attn_ln1_b, L0_attn_ln2_w, L0_attn_ln2_b, L0_attn_time_decay, L0_attn_time_first, L0_attn_time_mix_k, L0_attn_time_mix_v, L0_attn_time_mix_r, L0_attn_w_key, L0_attn_w_value, L0_attn_w_recept, L0_attn_w_output, L0_attn_f_time_mix_k, L0_attn_f_time_mix_r, L0_attn_f_w_key, L0_attn_f_w_recept, L0_attn_f_w_value, L0_ffn_W1, L0_ffn_b1, L0_ffn_W2, L0_ffn_b2, L0_c, L0_wmod, L1_attn_Wq, L1_attn_bq, L1_attn_Wk, L1_attn_bk, L1_attn_Wv, L1_attn_bv, L1_attn_Wo, L1_attn_bo, L1_ffn_W_router, L1_ffn_b_router, L1_ffn_W1, L1_ffn_b1, L1_ffn_W2, L1_ffn_b2, L1_c, L1_wmod):

    def _L0_attn_ref(x, ln1_w, ln1_b, ln2_w, ln2_b, time_decay, time_first, time_mix_k, time_mix_v, time_mix_r, w_key, w_value, w_recept, w_output, f_time_mix_k, f_time_mix_r, f_w_key, f_w_recept, f_w_value):
        import jax, jax.numpy as jnp
        import numpy as np
        B, T, D = (4, 512, 128)
        F = 4 * D
        EPS_INIT = -1e+30

        def layer_norm(x, w, b, eps=1e-05):
            mu = jnp.mean(x, axis=-1, keepdims=True)
            var = jnp.var(x, axis=-1, keepdims=True)
            return (x - mu) * jax.lax.rsqrt(var + eps) * w + b

        def time_shift(x):
            return jnp.concatenate([jnp.zeros_like(x[:, :1]), x[:, :-1]], axis=1)

        def wkv(w, u, k, v):
            bsz, _, dim = k.shape
            alpha0 = jnp.zeros((bsz, dim), k.dtype)
            beta0 = jnp.zeros((bsz, dim), k.dtype)
            eps0 = jnp.full((bsz, dim), EPS_INIT, k.dtype)

            def step(carry, kv_t):
                alpha, beta, eps = carry
                kt, vt = kv_t
                ukt = u + kt
                tau = jnp.maximum(ukt, eps)
                e1 = jnp.exp(eps - tau)
                e2 = jnp.exp(ukt - tau)
                out = (e1 * alpha + e2 * vt) / (e1 * beta + e2)
                weps = eps - w
                tau2 = jnp.maximum(weps, kt)
                d1 = jnp.exp(weps - tau2)
                d2 = jnp.exp(kt - tau2)
                return ((d1 * alpha + d2 * vt, d1 * beta + d2, tau2), out)
            kT = jnp.swapaxes(k, 0, 1)
            vT = jnp.swapaxes(v, 0, 1)
            _, outT = jax.lax.scan(step, (alpha0, beta0, eps0), (kT, vT))
            return jnp.swapaxes(outT, 0, 1)
        xn = layer_norm(x, ln1_w, ln1_b)
        lx = time_shift(xn)
        k = (xn * time_mix_k + lx * (1.0 - time_mix_k)) @ w_key
        v = (xn * time_mix_v + lx * (1.0 - time_mix_v)) @ w_value
        r = (xn * time_mix_r + lx * (1.0 - time_mix_r)) @ w_recept
        sr = jax.nn.sigmoid(r)
        w = jnp.exp(time_decay)
        out = wkv(w, time_first, k, v)
        x = x + out * sr @ w_output
        xn2 = layer_norm(x, ln2_w, ln2_b)
        lx2 = time_shift(xn2)
        fk = (xn2 * f_time_mix_k + lx2 * (1.0 - f_time_mix_k)) @ f_w_key
        fr = (xn2 * f_time_mix_r + lx2 * (1.0 - f_time_mix_r)) @ f_w_recept
        vk = jnp.square(jax.nn.relu(fk)) @ f_w_value
        x = x + jax.nn.sigmoid(fr) * vk
        return x

    def _L0_ffn_ref(hidden_states, W1, b1, W2, b2):
        import jax, jax.numpy as jnp
        import numpy as np
        HIDDEN = 128
        INTER = 512
        h = jax.nn.relu(jnp.einsum('bsh,hi->bsi', hidden_states, W1) + b1)
        return jnp.einsum('bsi,ih->bsh', h, W2) + b2

    def _L1_attn_ref(hidden_states, Wq, bq, Wk, bk, Wv, bv, Wo, bo):
        import jax, jax.numpy as jnp
        import numpy as np
        DIM, H, G = (128, 16, 4)
        HD = DIM // H
        HKV = H // G

        def rotate_half(x):
            return jnp.concatenate([-x[..., 1::2], x[..., ::2]], axis=-1)

        def rope_tables(seq_len, dim, dtype):
            inv_freq = 1.0 / 10000.0 ** (jnp.arange(0, dim, 2, dtype=jnp.float32) / dim)
            pos = jnp.arange(seq_len, dtype=jnp.float32)
            sinusoid = pos[:, None] * inv_freq[None, :]
            sin = jnp.concatenate([jnp.sin(sinusoid)] * 2, -1)
            cos = jnp.concatenate([jnp.cos(sinusoid)] * 2, -1)
            return (sin.astype(dtype)[None, :, None, :], cos.astype(dtype)[None, :, None, :])
        b, t, _ = hidden_states.shape
        q = (hidden_states @ Wq.T + bq).reshape(b, t, H, HD)
        k = (hidden_states @ Wk.T + bk).reshape(b, t, HKV, HD)
        v = (hidden_states @ Wv.T + bv).reshape(b, t, HKV, HD)
        sin, cos = rope_tables(t, HD, q.dtype)
        q = q * cos + rotate_half(q) * sin
        k = k * cos + rotate_half(k) * sin
        k = jnp.repeat(k, G, axis=2)
        v = jnp.repeat(v, G, axis=2)
        scale = 1.0 / jnp.sqrt(jnp.float32(HD)).astype(q.dtype)
        scores = jnp.einsum('bthd,bshd->btsh', q, k) * scale
        probs = jax.nn.softmax(scores, axis=2)
        context = jnp.einsum('btsh,bshd->bthd', probs, v).reshape(b, t, DIM)
        return context @ Wo.T + bo

    def _L1_ffn_ref(x, W_router, b_router, W1, b1, W2, b2):
        import jax, jax.numpy as jnp
        import numpy as np
        N_EMBD = 128
        NUM_EXPERTS = 8
        TOP_K = 2
        D_FF = 4 * N_EMBD
        B, S = (4, 256)
        Bv, Sv, D = x.shape
        flat_x = x.reshape(-1, D)
        T = flat_x.shape[0]
        logits = flat_x @ W_router + b_router
        top_vals, top_idx = jax.lax.top_k(logits, TOP_K)
        neg_inf = jnp.full_like(logits, -jnp.inf)
        sparse_logits = neg_inf.at[jnp.arange(T)[:, None], top_idx].set(top_vals)
        router_weights = jax.nn.softmax(sparse_logits, axis=-1)
        final_output = jnp.zeros_like(flat_x)
        for e in range(NUM_EXPERTS):
            expert_mask = jnp.any(top_idx == e, axis=-1)
            h = jax.nn.relu(flat_x @ W1[e] + b1[e])
            y = h @ W2[e] + b2[e]
            w = router_weights[:, e] * expert_mask.astype(x.dtype)
            final_output = final_output + y * w[:, None]
        return final_output.reshape(Bv, Sv, D)
    x = L0_attn_x
    mod = (_silu(L0_c) @ L0_wmod).reshape(L0_c.shape[0], 6, 1, -1)
    sa, ca, ga, sb, cb, gb = (mod[:, 0], mod[:, 1], mod[:, 2], mod[:, 3], mod[:, 4], mod[:, 5])
    ga = (2 * (ga >= 0) - 1) * jnp.maximum(jnp.abs(ga), 0.25)
    gb = (2 * (gb >= 0) - 1) * jnp.maximum(jnp.abs(gb), 0.25)
    h = _layernorm(x, axis=-1) * (1 + ca) + sa
    x = x + ga * _L0_attn_ref(h, L0_attn_ln1_w, L0_attn_ln1_b, L0_attn_ln2_w, L0_attn_ln2_b, L0_attn_time_decay, L0_attn_time_first, L0_attn_time_mix_k, L0_attn_time_mix_v, L0_attn_time_mix_r, L0_attn_w_key, L0_attn_w_value, L0_attn_w_recept, L0_attn_w_output, L0_attn_f_time_mix_k, L0_attn_f_time_mix_r, L0_attn_f_w_key, L0_attn_f_w_recept, L0_attn_f_w_value)
    h = _layernorm(x, axis=-1) * (1 + cb) + sb
    x = x + gb * _L0_ffn_ref(h, L0_ffn_W1, L0_ffn_b1, L0_ffn_W2, L0_ffn_b2)
    mod = (_silu(L1_c) @ L1_wmod).reshape(L1_c.shape[0], 6, 1, -1)
    sa, ca, ga, sb, cb, gb = (mod[:, 0], mod[:, 1], mod[:, 2], mod[:, 3], mod[:, 4], mod[:, 5])
    ga = (2 * (ga >= 0) - 1) * jnp.maximum(jnp.abs(ga), 0.25)
    gb = (2 * (gb >= 0) - 1) * jnp.maximum(jnp.abs(gb), 0.25)
    h = _layernorm(x, axis=-1) * (1 + ca) + sa
    x = x + ga * _L1_attn_ref(h, L1_attn_Wq, L1_attn_bq, L1_attn_Wk, L1_attn_bk, L1_attn_Wv, L1_attn_bv, L1_attn_Wo, L1_attn_bo)
    h = _layernorm(x, axis=-1) * (1 + cb) + sb
    x = x + gb * _L1_ffn_ref(h, L1_ffn_W_router, L1_ffn_b_router, L1_ffn_W1, L1_ffn_b1, L1_ffn_W2, L1_ffn_b2)
    return x

_drawn_inputs = setup_inputs


def setup_inputs(seed=0):
    import zlib

    import numpy as np

    out = dict(_drawn_inputs(seed))
    spreads = {'L0_attn_ln1_w': (1.0, 0.6),
     'L0_attn_ln1_b': (0.0, 0.8),
     'L0_attn_ln2_w': (1.0, 0.6),
     'L0_attn_ln2_b': (0.0, 0.8),
     'L1_attn_bq': (0.0, 2.0),
     'L1_attn_bk': (0.0, 2.0),
     'L1_attn_bv': (0.0, 2.0),
     'L1_attn_bo': (0.0, 2.0),
     'L1_ffn_b_router': (0.0, 2.0),
     'L1_ffn_b1': (0.0, 2.0),
     'L1_ffn_b2': (0.0, 2.0)}
    factors = {'L0_attn_time_decay': 8.0,
     'L0_attn_time_first': 8.0,
     'L0_attn_time_mix_k': 8.0,
     'L0_attn_time_mix_v': 8.0,
     'L0_attn_time_mix_r': 8.0,
     'L0_attn_w_key': 8.0,
     'L0_attn_w_value': 8.0,
     'L0_attn_w_recept': 8.0,
     'L0_attn_w_output': 8.0,
     'L0_attn_f_time_mix_k': 8.0,
     'L0_attn_f_time_mix_r': 8.0,
     'L0_attn_f_w_key': 8.0,
     'L0_attn_f_w_recept': 8.0,
     'L0_attn_f_w_value': 8.0,
     'L0_ffn_b1': 64.0,
     'L0_ffn_b2': 200.0,
     'L1_attn_Wq': 64.0,
     'L1_attn_Wk': 64.0,
     'L1_attn_Wv': 64.0,
     'L1_attn_Wo': 55.824,
     'L0_ffn_W1': 8.0,
     'L0_ffn_W2': 8.0,
     'L1_ffn_W_router': 8.0,
     'L1_ffn_W1': 8.0,
     'L1_ffn_W2': 8.0,
     'L1_c': 8.0,
     'L1_wmod': 8.0}
    for name, (base, spread) in spreads.items():
        noise = np.random.default_rng([zlib.crc32(name.encode()), seed]).standard_normal(out[name].shape)
        drawn = base * np.exp(spread * noise) if base else spread * noise
        out[name] = jnp.asarray(drawn.astype(out[name].dtype))
    for name, factor in factors.items():
        out[name] = (out[name] * factor).astype(out[name].dtype)
    return out
```

```python
from contextlib import ExitStack

import numpy as np

import concourse.bass as bass
from concourse import mybir

F32 = mybir.dt.float32
BF16 = mybir.dt.bfloat16
ALU = mybir.AluOpType
ACT = mybir.ActivationFunctionType
AX_X = mybir.AxisListType.X

P = 128
D = 128
B, T = 32, 256
BC = 2
N = BC * T
NT = N // P
CHUNKS = B // BC
FC = 4
H, KV, HD = 16, 4, 8
G = H // KV
EXPERTS = 8
PARTS = 3
SROWS = PARTS * PARTS * HD
KROWS = SROWS + PARTS
EPS = 1e-5
NEG_INIT = -1e30
SCALE = float(HD) ** -0.5
STAGES = 4

(LN1W, LN1B, LN2W, LN2B, DECAY, FIRST, MIXK, MIXV, MIXR, FMIXK, FMIXR, BQ, BK, L0B1) = list(range(13)) + [13]
NCOL = L0B1 + FC
CB0, SB0, CA1, SA1, CB1, SB1 = range(6)
SA, CA, GA, SB, CB, GB = range(6)

EVENTS = """
a_ld a_ldm a_var a_rstd a_norm a_h0 a_h a_tp a_xn a_dx a_xk a_xv a_xr a_r a_th a_k a_v a_m a_exp a_att a_wo
a_x1 a_fk a_rl a_sq a_fr a_th2 a_vk a_y a_st a_vec a_scl a_pol
b_ld b_ldm b_var b_rstd b_norm b_tp b_h b_w1 b_hs b_w2 b_x2 b_st b_q b_t b_v b_va b_qk b_p b_r b_st2 b_vec b_scl
c_ldq c_ldv c_ldm c_s c_mx c_mp c_mt c_mT c_rows c_s2 c_p c_pv c_o c_ot c_ctx c_ct c_cT c_wo c_y c_st c_vec
d_ld d_ldm d_var d_rstd d_norm d_tp d_h d_lg d_dm d_e d_wt d_w1 d_hs d_w2 d_acc d_st d_vec d_out
""".split()


class Count:

    def __init__(self, eng, sem):
        self.eng, self.sem, self.n = eng, sem, 0

    def __call__(self, ins):
        ins.then_inc(self.sem, 1)
        self.n += 1
        return self.n

    def wait(self, n=None):
        self.eng.wait_ge(self.sem, self.n if n is None else n)


def program(nc, a):
    ctx = ExitStack()
    with ctx:
        def sb(name, shape, dt=F32):
            return ctx.enter_context(nc.sbuf_tensor(name, shape, dt))

        def scratch(name, shape, dt=F32):
            return nc.dram_tensor(name, shape, dt).ap()

        bank = [ctx.enter_context(nc.psum_tensor(f"bank{n}", [P, 512], F32)) for n in range(8)]
        AB, CS, CO, DH, DY = bank[0:2], bank[2:4], bank[4], bank[5:7], bank[7]

        x_a = scratch("x_a", [B * T, D])
        x_b = scratch("x_b", [B * T, D])
        x_c = scratch("x_c", [B * T, D])
        q_parts = scratch("q_parts", [CHUNKS * P, PARTS * N], BF16)
        k_parts = scratch("k_parts", [CHUNKS * KV * HD, PARTS * N], BF16)
        v_tiles = scratch("v_tiles", [CHUNKS * P, NT * KV * 32])
        rows0 = scratch("rows0", [B, 6 * D])
        rows1 = scratch("rows1", [B, 6 * D])
        cols_mod = scratch("cols_mod", [P, B * 6])

        ident = sb("ident", [P, P])
        identb = sb("identb", [P, P], BF16)
        cos = sb("cos", [P, T])
        sin = sb("sin", [P, T])
        col = sb("col", [P, NCOL])
        negw = sb("negw", [P, 1])
        half = sb("half", [P, NT])
        wk, wv, wr, wo = (sb(n, [P, D]) for n in ("wk", "wv", "wr", "wo"))
        fwk = sb("fwk", [P, FC * P])
        fwr = sb("fwr", [P, D])
        fwv = sb("fwv", [P, FC, D])
        w1 = sb("w1", [P, FC * P])
        w2 = sb("w2", [P, FC, D])
        wqT, wqrT, wkT, wkrT = (sb(n, [P, P]) for n in ("wqT", "wqrT", "wkT", "wkrT"))
        bqr = sb("bqr", [P, 1])
        bkr = sb("bkr", [P, 1])
        wvT = sb("wvT", [P, KV * HD])
        woT = sb("woT", [P, D])
        bv = sb("bv", [P, KV * HD])
        wrt = sb("wrt", [P, EXPERTS])
        brt = sb("brt", [P, EXPERTS])
        rev = sb("rev", [P, EXPERTS])
        e1w = sb("e1w", [P, EXPERTS, FC * P])
        e2w = sb("e2w", [P, EXPERTS, FC, D])
        e1b = sb("e1b", [P, EXPERTS * FC])
        ones3 = sb("ones3", [PARTS, P], BF16)
        brow = sb("brow", [PARTS, (EXPERTS + 2) * D], BF16)
        BO, B2 = EXPERTS, EXPERTS + 1

        ax = sb("ax", [P, NT, D])
        am = sb("am", [P, BC, 3, D])
        ast = sb("ast", [P, NT, 6])
        amv = sb("amv", [P, NT, 2])
        avar = sb("avar", [P, NT])
        ars = sb("ars", [P, NT])
        az = sb("az", [P, NT, D])
        ah0 = sb("ah0", [P, NT, D])
        ah = sb("ah", [P, NT, D])
        axn = sb("axn", [P, BC, T + 1])
        adx = sb("adx", [P, BC, T])
        axk, axv, axr = (sb(n, [P, BC, T]) for n in ("axk", "axv", "axr"))
        ath = sb("ath", [P, N])
        aE = sb("aE", [P, BC, T + 1])
        wkv = sb("wkv", [P, 2 * FC, N])
        arl, asq = wkv[:, 0:FC, :], wkv[:, FC:2 * FC, :]
        azy, amx, amn, aP = (wkv[:, 2 * k:2 * k + 2, :].rearrange("p s (b t) -> p s b t", b=BC) for k in range(4))
        ards, aatt = wkv[:, 0, :], wkv[:, 1, :]
        aQ = sb("aQ", [P, 3, BC, T])
        ad2v = wkv[:, 2, :].rearrange("p (b t) -> p b t", b=BC)
        aAB = sb("aAB", [P, 2, BC, T + 1])
        and1 = sb("and1", [P, 2, BC, T])
        and2 = sb("and2", [P, 2, BC, T])
        aw = adx[:, :, :].rearrange("p b t -> p (b t)")
        ax1 = ah0
        ath2, aq = (aQ[:, k, :, :].rearrange("p b t -> p (b t)") for k in range(2))
        ay0, ay1, axo = (w_.rearrange("p b (t d) -> p (b t) d", d=D) for w_ in
                         (aQ[:, 2, :, :], and1[:, 0, :, :], and1[:, 1, :, :]))

        bx = sb("bx", [P, NT, D])
        bm = sb("bm", [P, BC, D])
        bc = sb("bc", [P, BC, 6])
        bst = sb("bst", [P, NT, 6])
        bmv = sb("bmv", [P, NT, 2])
        bvar = sb("bvar", [P, NT])
        brs = sb("brs", [P, NT])
        bz = sb("bz", [P, NT, D])
        bh = sb("bh", [P, N])
        bhs = sb("bhs", [P, FC, N])
        by = bz
        bx2 = sb("bx2", [P, NT, D])
        bt1, bt2, br1, br2 = bhs[:, 0, :], bhs[:, 1, :], bhs[:, 2:4, :], bhs[:, 0:2, :]
        bqk = sb("bqk", [P, 2, N])
        bp = sb("bp", [P, PARTS, 2, N], BF16)
        bva = sb("bva", [P, NT, KV, 32])

        cQ = sb("cQ", [P, H, N], BF16)
        cK = sb("cK", [P, KV, N], BF16)
        cV = sb("cV", [P, NT, KV, 32])
        cx = sb("cx", [P, NT, D])
        cm = sb("cm", [P, BC, D])
        cmx = sb("cmx", [P, NT, H])
        cmp = sb("cmp", [P, NT, PARTS, H], BF16)
        cr1 = sb("cr1", [P, NT, H])
        cr2 = sb("cr2", [P, NT, H])
        cmT = sb("cmT", [PARTS * H, N], BF16)
        cP = sb("cP", [P, 8, N])
        cos_ = sb("cos_", [P, N])
        crs = sb("crs", [P, 4, KV])
        cctx = sb("cctx", [P, NT, KV, 2, 2, HD])
        ccT = sb("ccT", [P, N])
        cy, cxo = (cP[:, k, :].rearrange("p (t d) -> p t d", d=D) for k in range(2))

        dx = sb("dx", [P, NT, D])
        dm = sb("dm", [P, BC, D])
        dc = sb("dc", [P, BC, 6])
        dst = sb("dst", [P, NT, 6])
        dmv = sb("dmv", [P, NT, 2])
        dvar = sb("dvar", [P, NT])
        drs = sb("drs", [P, NT])
        dz = sb("dz", [P, NT, D])
        dh = sb("dh", [P, N])
        dlg, deq, doh1, dlg2, doh2, dw1, dwt = (sb(n, [P, NT, EXPERTS]) for n in
                                                ("dlg", "deq", "doh1", "dlg2", "doh2", "dw1", "dwt"))
        dm1, dm2, di, ddm, de, dp1, dp2 = (sb(n, [P, NT]) for n in
                                           ("dm1", "dm2", "di", "ddm", "de", "dp1", "dp2"))
        dhs = sb("dhs", [P, 4, N])
        dacc = sb("dacc", [P, NT, D])
        dy, dxo = dz[:, :, :], dacc[:, :, :]

        sems = [ctx.enter_context(nc.semaphore(n)) for n in EVENTS]
        S = dict(zip(EVENTS, sems))
        span = range(sems[0].num, sems[-1].num + 1)
        assert len(span) == len(sems)

        def new_round():
            nc.all_engine_barrier()
            nc.gpsimd.sem_clear(span)
            nc.all_engine_barrier()

        def tiles(ap):
            return ap[:, :].rearrange("p (t d) -> p t d", t=NT)

        def per_batch(rows, like):
            return rows.unsqueeze(2).broadcast_to([P, BC, NT // BC, D])

        def by_batch(ap):
            return ap.rearrange("p (b t) d -> p b t d", b=BC)

        with nc.Block() as block:
            L, M, V2, V3, PW = S["a_ld"], S["a_ldm"], S["a_vec"], S["a_scl"], S["a_pol"]
            mm = S["a_k"]
            tc0 = arl[:, 0, 0:B]
            tc1 = arl[:, 0, B:2 * B]
            ec = arl[:, 0, 2 * B:4 * B]
            sc = arl[:, 0, 4 * B:6 * B]
            wmod0, wmod1 = asq[:, 0:2, :].rearrange("p a b -> p (a b)")[:, 0:6 * D], \
                asq[:, 2:4, :].rearrange("p a b -> p (a b)")[:, 0:6 * D]
            wq_n, wk_n = az[:, 0, :], az[0:KV * HD, 1, :]
            rq, rk = az[:, 2, :], az[0:KV * HD, 3, :]
            rowbuf = [cP[0:B, 0:2, :].rearrange("p a b -> p (a b)")[:, 0:6 * D],
                      cP[0:B, 2:4, :].rearrange("p a b -> p (a b)")[:, 0:6 * D]]
            rowneg = cP[0:B, 4, :]
            rowsgn = cP[0:B, 5, :]
            colbuf = cP[:, 6, 0:B * 6].rearrange("p (b s) -> p b s", s=6)
            NB = (EXPERTS + 2) * D
            braw = arl[0:PARTS, 1:4, :].rearrange("p a b -> p (a b)")[:, 0:NB]
            br_1 = bhs[0:PARTS, 0:3, :].rearrange("p a b -> p (a b)")[:, 0:NB]
            br_2 = dhs[0:PARTS, 0:3, :].rearrange("p a b -> p (a b)")[:, 0:NB]
            bpart = cQ[0:PARTS, 0:9, :].rearrange("p a b -> p (a b)")[:, 0:PARTS * NB] \
                .rearrange("p (s n) -> p s n", s=PARTS)
            mask3 = ax[0:PARTS, 0, 0:PARTS]
            bsum = [bhs[0:PARTS, 0:3, :].rearrange("p a b -> p (a b)")[:, 0:NB],
                    dhs[0:PARTS, 0:3, :].rearrange("p a b -> p (a b)")[:, 0:NB]]
            loads = [
                (ident[:, :], a["c_ident"]), (identb[:, :], a["c_identb"]), (cos[:, :], a["c_cos"]),
                (sin[:, :], a["c_sin"]), (col[:, :], a["cols"]), (wk[:, :], a["L0_attn_w_key"]),
                (wv[:, :], a["L0_attn_w_value"]), (wr[:, :], a["L0_attn_w_recept"]),
                (wo[:, :], a["L0_attn_w_output"]), (fwk[:, :], a["L0_attn_f_w_key"]),
                (fwr[:, :], a["L0_attn_f_w_recept"]),
                (fwv[:, :, :], a["L0_attn_f_w_value"].rearrange("(c p) d -> p c d", p=P)),
                (w1[:, :], a["L0_ffn_W1"]),
                (w2[:, :, :], a["L0_ffn_W2"].rearrange("(c p) d -> p c d", p=P)),
                (wqT[:, :], a["wqT"]), (wkT[:, :], a["wkT"]), (wvT[:, :], a["wvT"]), (woT[:, :], a["woT"]),
                (wq_n, a["L1_attn_Wq"]), (wk_n, a["L1_attn_Wk"]), (rq, a["c_rotq"]), (rk, a["c_rotk"]),
                (bv[:, :], a["L1_attn_bv"].partition_broadcast(P)),
                (wrt[:, :], a["L1_ffn_W_router"]), (brt[:, :], a["L1_ffn_b_router"].partition_broadcast(P)),
                (rev[:, :], a["c_rev"]), (e1b[:, :], a["e1b"]),
                (e1w[:, :, :], a["L1_ffn_W1"].rearrange("e p f -> p e f")),
                (e2w[:, :, :, :].rearrange("p e c d -> p (e c) d"),
                 a["L1_ffn_W2"].rearrange("e (c p) d -> p (e c) d", p=P)),
                (ones3[:, :], a["c_ones3"]), (mask3, a["c_mask3"]),
                (cK[SROWS:KROWS, :, :].rearrange("p g n -> p (g n)"), a["c_onesk"]),
                (tc0, a["cT0"]), (tc1, a["cT1"]), (wmod0, a["L0_wmod"]), (wmod1, a["L1_wmod"]),
                (braw, a["brow"].partition_broadcast(PARTS)),
            ]

            @block.sync
            def _(sp):
                for dst_, src_ in loads:
                    sp.dma_start(dst_, src_).then_inc(L, 16)
                sp.wait_ge(V2, ROWS_DONE)
                sp.dma_start(rows0, rowbuf[0]).then_inc(M, 16)
                sp.dma_start(rows1, rowbuf[1]).then_inc(M, 16)
                sp.dma_start(cols_mod, cP[:, 6, 0:B * 6]).then_inc(M, 16)
                sp.wait_ge(M, 48)

            ALL = 16 * len(loads)

            @block.gpsimd
            def _(pool):
                pool.memset(half[:, :], -0.5)
                pool.memset(axn[:, :, 0:1], 0.0)
                pool.memset(aE[:, :, 0:1], NEG_INIT)
                pool.memset(aAB[:, :, :, 0:1].rearrange("p a b o -> p (a b) o"), 0.0)
                pool.memset(bva[:, :, :, :].rearrange("p t g v -> p (t g v)"), 0.0).then_inc(PW, 1)
                pool.wait_ge(PW, 1)
                pool.memset(bva[:, :, :, 8:9].rearrange("p t g v -> p (t g) v"), 1.0).then_inc(PW, 1)

            @block.scalar
            def _(act):
                act.wait_ge(L, ALL)
                act.activation(negw[:, :], col[:, DECAY:DECAY + 1], ACT.Exp).then_inc(V3, 1)
                act.activation(ec, arl[:, 0, 0:2 * B], ACT.Exp, scale=-1.0).then_inc(V3, 1)

            @block.tensor
            def _(pe):
                pe.wait_ge(L, ALL)
                pe.matmul(bank[0][:, 0:P], wq_n, rq, start=True, stop=True)
                pe.matmul(bank[1][:, 0:P], wk_n, rk, start=True, stop=True)
                pe.matmul(bank[2][:, 0:1], rq, col[:, BQ:BQ + 1], start=True, stop=True)
                pe.matmul(bank[3][:, 0:1], rk, col[0:KV * HD, BK:BK + 1], start=True, stop=True).then_inc(mm, 1)
                pe.wait_ge(V2, 4)
                for l, wm in enumerate((wmod0, wmod1)):
                    s = sc[:, l * B:(l + 1) * B]
                    pe.matmul(bank[4 + 2 * l][0:B, 0:3 * D], s, wm[:, 0:3 * D], start=True, stop=True)
                    pe.matmul(bank[5 + 2 * l][0:B, 0:3 * D], s, wm[:, 3 * D:6 * D], start=True,
                              stop=True).then_inc(mm, 1)
                pe.wait_ge(V2, 8)
                for j, (l, kind) in enumerate(((0, CB), (0, SB), (1, CA), (1, SA), (1, CB), (1, SB))):
                    wm = (wmod0, wmod1)[l]
                    pe.matmul(bank[j // 3][:, (j % 3) * 128:(j % 3) * 128 + B], wm[:, kind * D:(kind + 1) * D],
                              sc[:, l * B:(l + 1) * B], start=True, stop=True).then_inc(mm, 1)

            @block.vector
            def _(dve):
                c = Count(dve, V2)
                dve.wait_ge(L, ALL)
                dve.wait_ge(V3, 2)
                c(dve.tensor_scalar(negw[:, :], negw[:, :], -1.0, None, ALU.mult))
                c(dve.tensor_scalar(ec, ec, 1.0, None, ALU.add))
                c.wait()
                c(dve.reciprocal(ec, ec))
                c.wait()
                c(dve.tensor_tensor(sc, arl[:, 0, 0:2 * B], ec, ALU.mult))
                dve.wait_ge(mm, 1)
                c(dve.tensor_copy(wqrT[:, :], bank[0][:, 0:P]))
                c(dve.tensor_copy(wkrT[:, :], bank[1][:, 0:P]))
                c(dve.tensor_copy(bqr[:, :], bank[2][:, 0:1]))
                c(dve.tensor_copy(bkr[:, :], bank[3][:, 0:1]))
                c(dve.tensor_scalar(wo[:, :], wo[:, :], 0.5, None, ALU.mult))
                c(dve.tensor_scalar(fwv[:, :, :], fwv[:, :, :], 0.5, None, ALU.mult))
                for l in range(2):
                    dve.wait_ge(mm, 2 + l)
                    rb = rowbuf[l]
                    for j in range(6):
                        src_ = bank[4 + 2 * l + j // 3][0:B, (j % 3) * D:(j % 3 + 1) * D]
                        out_ = rb[:, j * D:(j + 1) * D]
                        if j in (SA, SB):
                            c(dve.tensor_copy(out_, src_))
                        elif j in (CA, CB):
                            c(dve.tensor_scalar(out_, src_, 1.0, None, ALU.add))
                        else:
                            c(dve.tensor_scalar(rowneg[:, 0:D], src_, -1.0, 0.25, ALU.mult, ALU.max))
                            c(dve.tensor_scalar(rowsgn[:, 0:D], src_, 0.0, 2.0, ALU.is_ge, ALU.mult))
                            c.wait()
                            c(dve.tensor_tensor(rowneg[:, 0:D], src_, rowneg[:, 0:D], ALU.max))
                            c.wait()
                            c(dve.scalar_tensor_tensor(out_, rowsgn[:, 0:D], -1.0, rowneg[:, 0:D],
                                                       ALU.add, ALU.mult))
                            c.wait()
                for j in range(6):
                    dve.wait_ge(mm, 6 if j < 3 else 9)
                    src_ = bank[j // 3][:, (j % 3) * 128:(j % 3) * 128 + B]
                    c(dve.tensor_scalar(colbuf[:, :, j], src_, 0.0 if j % 2 else 1.0, None, ALU.add))
                assert c.n == ROWS_DONE, c.n
                c(dve.tensor_copy(bpart[:, 0, :], braw))
                c.wait()
                c(dve.tensor_tensor(br_1, braw, bpart[:, 0, :], ALU.subtract))
                c.wait()
                c(dve.tensor_copy(bpart[:, 1, :], br_1))
                c.wait()
                c(dve.tensor_tensor(br_2, br_1, bpart[:, 1, :], ALU.subtract))
                c.wait()
                c(dve.tensor_copy(bpart[:, 2, :], br_2))
                c.wait()
                c(dve.tensor_scalar(bsum[0], bpart[:, 0, :], mask3[:, 0:1], None, ALU.mult))
                c.wait()
                c(dve.scalar_tensor_tensor(bsum[1], bpart[:, 1, :], mask3[:, 1:2], bsum[0], ALU.mult, ALU.add))
                c.wait()
                c(dve.scalar_tensor_tensor(brow[:, :], bpart[:, 2, :], mask3[:, 2:3], bsum[1], ALU.mult, ALU.add))
                c.wait()

        new_round()

        def one_round(n, live):
            on = dict(zip("ABCD", live))
            order = [s for s in SCHEDULE if on[s[0]]]
            ca, cb, cc, cd = n, n - 1, n - 2, n - 3

            def rows(dram, i):
                return dram[bass.ds(i * N, N), :].rearrange("(t p) d -> p t d", p=P)

            def row_mod(dram, i, k0, k):
                return dram[bass.ds(i * BC, BC), k0 * D:(k0 + k) * D].partition_broadcast(P)

            with nc.Block() as block:
                @block.sync
                def _(sp):
                    if on["D"]:
                        sp.dma_start(dx[:, :, :], rows(x_c, cd)).then_inc(S["d_ld"], 16)
                        sp.dma_start(dc[:, :, :].rearrange("p b s -> p (b s)"),
                                     cols_mod[:, bass.ds(cd * BC * 6, BC * 6)]).then_inc(S["d_ldm"], 16)
                        sp.dma_start(dm[:, :, :], row_mod(rows1, cd, GB, 1)).then_inc(S["d_ldm"], 16)
                    if on["A"]:
                        sp.dma_start(ax[:, :, :], rows(a["x"], ca)).then_inc(S["a_ld"], 16)
                        sp.dma_start(am[:, :, :, :].rearrange("p b s d -> p b (s d)"),
                                     row_mod(rows0, ca, SA, 3)).then_inc(S["a_ldm"], 16)
                    if on["C"]:
                        for i in range(PARTS):
                            for j in range(PARTS):
                                r0 = (i * PARTS + j) * HD
                                sp.dma_start(cQ[r0:r0 + HD, :, :],
                                             q_parts[bass.ds(cc * P, P), i * N:(i + 1) * N]
                                             .rearrange("(h d) t -> d h t", d=HD)).then_inc(S["c_ldq"], 16)
                                sp.dma_start(cK[r0:r0 + HD, :, :],
                                             k_parts[bass.ds(cc * KV * HD, KV * HD), j * N:(j + 1) * N]
                                             .rearrange("(g d) t -> d g t", d=HD)).then_inc(S["c_ldq"], 16)
                        sp.dma_start(cV[:, :, :, :].rearrange("p t g v -> p (t g v)"),
                                     v_tiles[bass.ds(cc * P, P), :]).then_inc(S["c_ldv"], 16)
                        sp.dma_start(cx[:, :, :], rows(x_b, cc)).then_inc(S["c_ldm"], 16)
                        sp.dma_start(cm[:, :, :], row_mod(rows1, cc, GA, 1)).then_inc(S["c_ldm"], 16)
                    if on["B"]:
                        sp.dma_start(bx[:, :, :], rows(x_a, cb)).then_inc(S["b_ld"], 16)
                        sp.dma_start(bc[:, :, :].rearrange("p b s -> p (b s)"),
                                     cols_mod[:, bass.ds(cb * BC * 6, BC * 6)]).then_inc(S["b_ldm"], 16)
                        sp.dma_start(bm[:, :, :], row_mod(rows0, cb, GB, 1)).then_inc(S["b_ldm"], 16)
                    for s in order:
                        if s == "A_out":
                            sp.wait_ge(S["a_y"], 3)
                            sp.dma_start(rows(x_a, ca), axo).then_inc(S["a_st"], 16)
                        if s == "B_w2":
                            sp.wait_ge(S["b_x2"], 1)
                            sp.dma_start(rows(x_b, cb), bx2[:, :, :]).then_inc(S["b_st"], 16)
                        if s == "B_split":
                            sp.wait_ge(S["b_va"], 1)
                            sp.dma_start(v_tiles[bass.ds(cb * P, P), :],
                                         bva[:, :, :, :].rearrange("p t g v -> p (t g v)")).then_inc(S["b_st2"], 16)
                            sp.wait_ge(S["b_p"], 3)
                            sp.dma_start(q_parts[bass.ds(cb * P, P), :].rearrange("p (s n) -> p s n", s=PARTS),
                                         bp[:, :, 0, :]).then_inc(S["b_st2"], 16)
                            sp.dma_start(k_parts[bass.ds(cb * KV * HD, KV * HD), :]
                                         .rearrange("p (s n) -> p s n", s=PARTS),
                                         bp[0:KV * HD, :, 1, :]).then_inc(S["b_st2"], 16)
                        if s == "C_max":
                            sp.wait_ge(S["c_mT"], 1)
                            for i in range(PARTS):
                                sp.dma_start(cQ[SROWS + i:SROWS + i + 1, :, :],
                                             cmT[i * H:(i + 1) * H, :]).then_inc(S["c_rows"], 16)
                        if s == "C_fin":
                            sp.wait_ge(S["c_y"], 1)
                            sp.dma_start(rows(x_c, cc), cxo).then_inc(S["c_st"], 16)
                    if on["D"]:
                        sp.wait_ge(S["d_out"], 1)
                        sp.dma_start(rows(a["out"], cd), dxo).then_inc(S["d_st"], 16)
                    if on["A"]:
                        sp.wait_ge(S["a_st"], 16)
                    if on["B"]:
                        sp.wait_ge(S["b_st"], 16)
                        sp.wait_ge(S["b_st2"], 48)
                    if on["C"]:
                        sp.wait_ge(S["c_st"], 16)
                    if on["D"]:
                        sp.wait_ge(S["d_st"], 16)

                @block.gpsimd
                def _(pool):
                    def rstd(k, var, nth, out):
                        pool.wait_ge(S[k + "_var"], nth)
                        pool.tensor_tensor(out[:, :], var[:, :], half[:, :], ALU.pow).then_inc(S[k + "_rstd"], 1)

                    def diff(nth):
                        pool.wait_ge(S["a_xn"], nth)
                        if nth == 2:
                            pool.wait_ge(S["a_xr"], 1)
                        pool.tensor_tensor(adx[:, :, :], axn[:, :, 1:T + 1], axn[:, :, 0:T],
                                           ALU.subtract).then_inc(S["a_dx"], 1)

                    for s in order:
                        if s == "A_ln0":
                            rstd("a", avar, 1, ars)
                            pool.wait_ge(S["a_h0"], 1)
                            pool.wait_ge(S["a_ldm"], 16)
                            pool.tensor_tensor(by_batch(ah[:, :, :]), by_batch(ah0[:, :, :]),
                                               per_batch(am[:, :, SA, :], ah), ALU.add).then_inc(S["a_h"], 1)
                        if s == "A_ln1":
                            rstd("a", avar, 2, ars)
                        if s == "A_xn":
                            diff(1)
                        if s == "A_ln2":
                            rstd("a", avar, 3, ars)
                        if s == "A_xn2":
                            diff(2)
                        if s == "A_out":
                            pool.wait_ge(S["a_y"], 1)
                            pool.tensor_tensor(by_batch(ay1), by_batch(ay0),
                                               per_batch(am[:, :, GA, :], ay0), ALU.mult).then_inc(S["a_y"], 1)
                            pool.wait_ge(S["a_y"], 2)
                            pool.tensor_tensor(axo, ay1, ax[:, :, :], ALU.add).then_inc(S["a_y"], 1)
                        if s == "B_ln0":
                            rstd("b", bvar, 1, brs)
                        if s == "B_ln1":
                            rstd("b", bvar, 2, brs)
                        if s == "B_split":
                            pool.wait_ge(S["b_p"], 1)
                            pool.wait_ge(S["b_qk"], 2)
                            pool.tensor_tensor(br1, bqk[:, :, :], bp[:, 0, :, :],
                                               ALU.subtract).then_inc(S["b_r"], 1)
                            pool.wait_ge(S["b_p"], 2)
                            pool.wait_ge(S["b_r"], 1)
                            pool.tensor_tensor(br2, br1, bp[:, 1, :, :],
                                               ALU.subtract).then_inc(S["b_r"], 1)
                        if s == "D_ln":
                            rstd("d", dvar, 1, drs)

                @block.scalar
                def _(act):
                    def feature_affine(k, nth, ps, out, c, cs, sh):
                        act.wait_ge(S[k + "_tp"], nth)
                        if nth == 1:
                            act.wait_ge(S[k + "_ldm"], 32)
                        for b in range(BC):
                            act.activation(out[:, b * T:(b + 1) * T], ps[:, b * T:(b + 1) * T], ACT.Identity,
                                           bias=c[:, b, sh:sh + 1], scale=c[:, b, cs:cs + 1]).then_inc(S[k + "_h"], 1)

                    for s in order:
                        if s in ("A_xn", "A_xn2"):
                            nth = 1 if s == "A_xn" else 2
                            w_, b_ = (LN1W, LN1B) if nth == 1 else (LN2W, LN2B)
                            act.wait_ge(S["a_tp"], nth)
                            src_ = AB[nth - 1]
                            act.activation(axn[:, :, 1:T + 1], src_[:, :].rearrange("p (b t) -> p b t", b=BC),
                                           ACT.Identity, bias=col[:, b_:b_ + 1],
                                           scale=col[:, w_:w_ + 1]).then_inc(S["a_xn"], 1)
                        if s == "A_rkv":
                            act.wait_ge(S["a_r"], 1)
                            act.activation(ath[:, :], AB[1][:, :], ACT.Tanh, scale=0.5).then_inc(S["a_th"], 1)
                            act.wait_ge(S["a_m"], 1)
                            act.activation(aP, amx, ACT.Exp, scale=-1.0).then_inc(S["a_exp"], 1)
                            act.wait_ge(S["a_m"], 2)
                            act.activation(aQ[:, 1:3, :, :], amn, ACT.Exp).then_inc(S["a_exp"], 1)
                        if s == "A_fk":
                            for c in range(FC):
                                act.wait_ge(S["a_fk"], c + 1)
                                act.activation(arl[:, c, :], AB[c % 2][:, :], ACT.Relu).then_inc(S["a_rl"], 1)
                                act.wait_ge(S["a_rl"], c + 1)
                                act.activation(asq[:, c, :], arl[:, c, :], ACT.Square).then_inc(S["a_sq"], 1)
                        if s == "A_fr":
                            act.wait_ge(S["a_fr"], 1)
                            act.activation(ath2, AB[0][:, :], ACT.Tanh, scale=0.5).then_inc(S["a_th2"], 1)
                        if s == "B_h":
                            feature_affine("b", 1, AB[0], bh, bc, CB0, SB0)
                        if s == "B_w1":
                            for c in range(FC):
                                act.wait_ge(S["b_w1"], c + 1)
                                act.activation(bhs[:, c, :], AB[(c + 1) % 2][:, :], ACT.Relu,
                                               bias=col[:, L0B1 + c:L0B1 + c + 1]).then_inc(S["b_hs"], 1)
                        if s == "B_h2":
                            feature_affine("b", 2, AB[0], bh, bc, CA1, SA1)
                        if s == "B_split":
                            act.wait_ge(S["b_qk"], 2)
                            act.activation(bp[:, 0, :, :], bqk[:, :, :], ACT.Copy).then_inc(S["b_p"], 1)
                            act.wait_ge(S["b_r"], 1)
                            act.activation(bp[:, 1, :, :], br1, ACT.Copy).then_inc(S["b_p"], 1)
                            act.wait_ge(S["b_r"], 2)
                            act.activation(bp[:, 2, :, :], br2, ACT.Copy).then_inc(S["b_p"], 1)
                        if s == "C_max":
                            act.wait_ge(S["c_mt"], 1)
                            act.activation(cmT[:, :], CO[0:PARTS * H, 0:N // 2].bitcast(BF16),
                                           ACT.Copy).then_inc(S["c_mT"], 1)
                        if s.startswith("C_g"):
                            g0 = int(s[3:])
                            for m in range(4 * g0, 4 * g0 + 4):
                                act.wait_ge(S["c_s2"], m + 1)
                                if m >= 8:
                                    act.wait_ge(S["c_pv"], (m - 8) // 4 + 1)
                                act.activation(cP[:, m % 8, :], CS[m % 2][:, :], ACT.Exp,
                                               scale=SCALE).then_inc(S["c_p"], 1)
                        if s.startswith("C_o"):
                            o = int(s[3:])
                            act.wait_ge(S["c_pv"], 2 * o + 2)
                            if o:
                                act.wait_ge(S["c_ot"], o)
                            act.activation(cos_[:, :], CO[:, :], ACT.Copy).then_inc(S["c_o"], 1)
                        if s == "C_fin":
                            act.wait_ge(S["c_ct"], 1)
                            act.activation(ccT[:, :], CO[:, :], ACT.Copy).then_inc(S["c_cT"], 1)
                        if s == "D_ln":
                            feature_affine("d", 1, DH[0], dh, dc, CB1, SB1)
                        if s == "D_router":
                            act.wait_ge(S["d_dm"], 1)
                            act.activation(de[:, :], ddm[:, :], ACT.Exp).then_inc(S["d_e"], 1)
                        if s.startswith("D_q"):
                            q = int(s[3:])
                            act.wait_ge(S["d_w1"], q + 1)
                            if q >= 4:
                                act.wait_ge(S["d_w2"], q - 3)
                            act.activation(dhs[:, q % 4, :], DH[q % 2][:, :], ACT.Relu,
                                           bias=e1b[:, q:q + 1]).then_inc(S["d_hs"], 1)

                @block.tensor
                def _(pe):
                    def turn(k, nth, src_, ps):
                        pe.wait_ge(S[k + "_norm"], NT * nth)
                        for t in range(NT):
                            ins = pe.transpose(ps[:, t * P:(t + 1) * P], src_[:, t, :], ident[:, :])
                        ins.then_inc(S[k + "_tp"], 1)

                    def bias_rows(ps, r):
                        pe.matmul(ps[:, :], ones3[:, :],
                                  brow[:, r * D:(r + 1) * D].unsqueeze(1).broadcast_to([PARTS, NT, D]),
                                  start=True, stop=False)

                    def expert_up(q):
                        e, c = divmod(q, FC)
                        pe.wait_ge(S["d_h"], 2)
                        if q >= 2:
                            pe.wait_ge(S["d_hs"], q - 1)
                        pe.matmul(DH[q % 2][:, :], e1w[:, e, c * P:(c + 1) * P], dh[:, :],
                                  start=True, stop=True).then_inc(S["d_w1"], 1)

                    def expert_down(q):
                        e, c = divmod(q, FC)
                        if c == 0:
                            if e:
                                pe.wait_ge(S["d_acc"], NT * e)
                            else:
                                pe.wait_ge(S["d_lg"], 1)
                            bias_rows(DY, e)
                        pe.wait_ge(S["d_hs"], q + 1)
                        for t in range(NT):
                            ins = pe.matmul(DY[:, t * P:(t + 1) * P], dhs[:, q % 4, t * P:(t + 1) * P],
                                            e2w[:, e, c, :], start=False, stop=(c == FC - 1 and t == NT - 1))
                        ins.then_inc(S["d_w2"], 1)

                    def weigh(g0):
                        if g0 % 2 == 0 and g0:
                            pe.wait_ge(S["c_ctx"], g0 // 2)
                        if g0 == 0:
                            pe.wait_ge(S["c_mT"], 1)
                            pe.wait_ge(S["c_ldv"], 16)
                        pe.wait_ge(S["c_p"], 4 * g0 + 4)
                        b, sc_ = g0 // 4, g0 % 2
                        for g in range(KV):
                            ins = pe.matmul(CO[32 * g:32 * g + 32, :], cV[:, b * 2 + sc_, g, :],
                                            cP[:, (4 * g0 + g) % 8, :], start=(sc_ == 0), stop=(sc_ == 1))
                        ins.then_inc(S["c_pv"], 1)

                    for s in order:
                        if s == "A_xn":
                            turn("a", 1, az, AB[0])
                        if s == "A_rkv":
                            pe.wait_ge(S["a_xr"], 1)
                            pe.matmul(AB[1][:, :], wr[:, :], axr[:, :, :].rearrange("p b t -> p (b t)"),
                                      start=True, stop=True).then_inc(S["a_r"], 1)
                            pe.wait_ge(S["a_xk"], 1)
                            pe.matmul(AB[0][:, :], wk[:, :], axk[:, :, :].rearrange("p b t -> p (b t)"),
                                      start=True, stop=True).then_inc(S["a_k"], 1)
                            pe.wait_ge(S["a_xv"], 1)
                            pe.wait_ge(S["a_th"], 1)
                            pe.matmul(AB[1][:, :], wv[:, :], axv[:, :, :].rearrange("p b t -> p (b t)"),
                                      start=True, stop=True).then_inc(S["a_v"], 1)
                        if s == "A_wo":
                            pe.wait_ge(S["a_att"], 1)
                            for t in range(NT):
                                ins = pe.matmul(AB[0][:, t * P:(t + 1) * P], aatt[:, t * P:(t + 1) * P], wo[:, :],
                                                start=True, stop=True)
                            ins.then_inc(S["a_wo"], 1)
                        if s == "A_xn2":
                            turn("a", 2, az, AB[1])
                        if s == "A_fk":
                            pe.wait_ge(S["a_xk"], 2)
                            for c in range(FC):
                                if c >= 2:
                                    pe.wait_ge(S["a_rl"], c - 1)
                                elif c == 1:
                                    pe.wait_ge(S["a_xn"], 2)
                                pe.matmul(AB[c % 2][:, :], fwk[:, c * P:(c + 1) * P],
                                          axk[:, :, :].rearrange("p b t -> p (b t)"),
                                          start=True, stop=True).then_inc(S["a_fk"], 1)
                        if s == "A_fr":
                            pe.wait_ge(S["a_xr"], 2)
                            pe.wait_ge(S["a_rl"], 3)
                            x_ = axr[:, :, :].rearrange("p b t -> p (b t)")
                            for t in range(NT):
                                ins = pe.matmul(AB[0][:, t * P:(t + 1) * P], x_[:, t * P:(t + 1) * P], fwr[:, :],
                                                start=True, stop=True)
                            ins.then_inc(S["a_fr"], 1)
                        if s == "A_vk":
                            pe.wait_ge(S["a_sq"], FC)
                            for t in range(NT):
                                for c in range(FC):
                                    ins = pe.matmul(AB[1][:, t * P:(t + 1) * P], asq[:, c, t * P:(t + 1) * P],
                                                    fwv[:, c, :], start=(c == 0), stop=(c == FC - 1))
                            ins.then_inc(S["a_vk"], 1)
                        if s == "B_h":
                            turn("b", 1, bz, AB[0])
                        if s == "B_w1":
                            pe.wait_ge(S["b_h"], 2)
                            for c in range(FC):
                                if c >= 2:
                                    pe.wait_ge(S["b_hs"], c - 1)
                                pe.matmul(AB[(c + 1) % 2][:, :], w1[:, c * P:(c + 1) * P], bh[:, :],
                                          start=True, stop=True).then_inc(S["b_w1"], 1)
                        if s == "B_w2":
                            pe.wait_ge(S["b_hs"], FC)
                            bias_rows(AB[1], B2)
                            for t in range(NT):
                                for c in range(FC):
                                    ins = pe.matmul(AB[1][:, t * P:(t + 1) * P], bhs[:, c, t * P:(t + 1) * P],
                                                    w2[:, c, :], start=False, stop=(c == FC - 1 and t == NT - 1))
                            ins.then_inc(S["b_w2"], 1)
                        if s == "B_h2":
                            turn("b", 2, bz, AB[0])
                        if s == "B_qk":
                            pe.wait_ge(S["b_h"], 4)
                            for j, (w_, wr_) in enumerate(((wqT, wqrT), (wkT, wkrT))):
                                if j:
                                    pe.wait_ge(S["b_t"], 1)
                                pe.matmul(AB[1][:, :], w_[:, :], bh[:, :], start=True, stop=True).then_inc(S["b_q"], 1)
                                if j:
                                    pe.wait_ge(S["b_t"], 2)
                                pe.matmul(AB[0][:, :], wr_[:, :], bh[:, :], start=True, stop=True).then_inc(S["b_q"], 1)
                            pe.wait_ge(S["b_t"], 3)
                            for t in range(NT):
                                ins = pe.matmul(AB[1][:, t * 32:(t + 1) * 32], bh[:, t * P:(t + 1) * P], wvT[:, :],
                                                start=True, stop=True)
                            ins.then_inc(S["b_v"], 1)
                        if s.startswith("C_s"):
                            u = int(s[3:])
                            if u == 0:
                                pe.wait_ge(S["c_ldq"], 16 * 2 * PARTS * PARTS)
                            if u >= 2:
                                pe.wait_ge(S["c_mx"], u - 1)
                            bt, hp = divmod(u, H // 2)
                            b = bt // 2
                            for j in range(2):
                                h = 2 * hp + j
                                ins = pe.matmul(CS[u % 2][:, j * T:(j + 1) * T],
                                                cQ[0:SROWS, h, bt * P:(bt + 1) * P],
                                                cK[0:SROWS, h // G, b * T:(b + 1) * T], start=True, stop=True)
                            ins.then_inc(S["c_s"], 1)
                        if s == "C_max":
                            pe.wait_ge(S["c_mp"], 3)
                            for t in range(NT):
                                ins = pe.transpose(CO[0:PARTS * H, t * 64:(t + 1) * 64].bitcast(BF16),
                                                   cmp[:, t, :, :].rearrange("p s h -> p (s h)"), identb[:, :])
                            ins.then_inc(S["c_mt"], 1)
                        if s.startswith("C_g"):
                            g0 = int(s[3:])
                            if g0 == 0:
                                pe.wait_ge(S["c_rows"], 16 * PARTS)
                                pe.wait_ge(S["c_mx"], 32)
                            bp_, sc_ = divmod(g0, 2)
                            b, pp = divmod(bp_, 2)
                            for g in range(KV):
                                m = 4 * g0 + g
                                if m >= 2:
                                    pe.wait_ge(S["c_p"], m - 1)
                                h0 = g * G + pp * 2
                                pe.matmul(CS[m % 2][:, :],
                                          cK[0:KROWS, g, b * T + sc_ * P:b * T + (sc_ + 1) * P],
                                          cQ[0:KROWS, h0:h0 + 2, b * T:(b + 1) * T],
                                          start=True, stop=True).then_inc(S["c_s2"], 1)
                            if g0:
                                weigh(g0 - 1)
                            if g0 == 7:
                                weigh(7)
                        if s.startswith("C_o"):
                            o = int(s[3:])
                            pe.wait_ge(S["c_o"], o + 1)
                            for j in range(4):
                                ins = pe.transpose(CO[:, j * P:(j + 1) * P], cos_[:, j * P:(j + 1) * P], ident[:, :])
                            ins.then_inc(S["c_ot"], 1)
                        if s == "C_fin":
                            pe.wait_ge(S["c_ctx"], 4)
                            for t in range(NT):
                                ins = pe.transpose(CO[:, t * P:(t + 1) * P],
                                                   cctx[:, t, :, :, :, :].rearrange("p g a b d -> p (g a b d)"),
                                                   ident[:, :])
                            ins.then_inc(S["c_ct"], 1)
                            pe.wait_ge(S["c_cT"], 1)
                            bias_rows(CS[0], BO)
                            for t in range(NT):
                                ins = pe.matmul(CS[0][:, t * P:(t + 1) * P], ccT[:, t * P:(t + 1) * P], woT[:, :],
                                                start=False, stop=(t == NT - 1))
                            ins.then_inc(S["c_wo"], 1)
                        if s == "D_ln":
                            turn("d", 1, dz, DH[0])
                        if s == "D_router":
                            pe.wait_ge(S["d_h"], 2)
                            for t in range(NT):
                                ins = pe.matmul(DY[:, t * EXPERTS:(t + 1) * EXPERTS], dh[:, t * P:(t + 1) * P],
                                                wrt[:, :], start=True, stop=True)
                            ins.then_inc(S["d_tp"], 1)
                            expert_up(0)
                        if s.startswith("D_q"):
                            q = int(s[3:])
                            if q + 1 < EXPERTS * FC:
                                expert_up(q + 1)
                            expert_down(q)

                @block.vector
                def _(dve):
                    av = Count(dve, S["a_vec"])
                    bv_ = Count(dve, S["b_vec"])
                    cv = Count(dve, S["c_vec"])
                    dv = Count(dve, S["d_vec"])

                    def stats(k, c, src_, st, mv, var, out_z, rs, nth):
                        for t in range(NT):
                            c(dve.bn_stats(st[:, t, :], src_[:, t, :]))
                        c.wait()
                        for t in range(NT):
                            c(dve.bn_aggr(mv[:, t, :], st[:, t, :]))
                        c.wait()
                        dve.tensor_scalar(var[:, :], mv[:, :, 1], EPS, None, ALU.add).then_inc(S[k + "_var"], 1)
                        dve.wait_ge(S[k + "_rstd"], nth)
                        for t in range(NT):
                            dve.tensor_scalar(out_z[:, t, :], src_[:, t, :], mv[:, t, 0:1], rs[:, t:t + 1],
                                              ALU.subtract, ALU.mult).then_inc(S[k + "_norm"], 1)

                    def mix(nth, which):
                        dve.wait_ge(S["a_dx"], nth)
                        for out_, m_, ev in which:
                            dve.scalar_tensor_tensor(out_[:, :, :], adx[:, :, :], col[:, m_:m_ + 1],
                                                     axn[:, :, 0:T], ALU.mult, ALU.add).then_inc(S[ev], 1)

                    k_ps = AB[0][:, :].rearrange("p (b t) -> p b t", b=BC)
                    v_ps = AB[1][:, :].rearrange("p (b t) -> p b t", b=BC)

                    def apart(x_):
                        return x_.rearrange("p (b t) -> p b t", b=BC)

                    def every(x_):
                        return x_[:, :].unsqueeze(1).broadcast_to([P, BC, T])

                    for s in order:
                        if s == "A_ln0":
                            dve.wait_ge(S["a_ld"], 16)
                            for t in range(NT):
                                av(dve.bn_stats(ast[:, t, :], ax[:, t, :]))
                            av.wait()
                            for t in range(NT):
                                av(dve.bn_aggr(amv[:, t, :], ast[:, t, :]))
                            av.wait()
                            dve.tensor_scalar(avar[:, :], amv[:, :, 1], EPS, None, ALU.add).then_inc(S["a_var"], 1)
                            dve.wait_ge(S["a_rstd"], 1)
                            for t in range(NT):
                                av(dve.tensor_scalar(az[:, t, :], ax[:, t, :], amv[:, t, 0:1], ars[:, t:t + 1],
                                                     ALU.subtract, ALU.mult))
                            av.wait()
                            dve.wait_ge(S["a_ldm"], 16)
                            dve.tensor_tensor(by_batch(ah0[:, :, :]), by_batch(az[:, :, :]),
                                              per_batch(am[:, :, CA, :], az), ALU.mult).then_inc(S["a_h0"], 1)
                        if s == "A_ln1":
                            dve.wait_ge(S["a_h"], 1)
                            dve.wait_ge(S["a_h0"], 1)
                            stats("a", av, ah, ast, amv, avar, az, ars, 2)
                        if s == "A_xn":
                            mix(1, ((axr, MIXR, "a_xr"), (axk, MIXK, "a_xk"), (axv, MIXV, "a_xv")))
                        if s == "A_rkv":
                            dve.wait_ge(S["a_k"], 1)
                            for b in range(BC):
                                av(dve.tensor_tensor_scan(aE[:, b, 1:T + 1], negw[:, 0:1].broadcast_to([P, T]),
                                                          k_ps[:, b, :], NEG_INIT, ALU.add, ALU.max))
                            av.wait()
                            av(dve.scalar_tensor_tensor(azy[:, 0, :, :], k_ps, col[:, FIRST:FIRST + 1],
                                                        aE[:, :, 0:T], ALU.add, ALU.subtract))
                            av(dve.scalar_tensor_tensor(azy[:, 1, :, :], aE[:, :, 0:T], negw[:, 0:1],
                                                        k_ps, ALU.add, ALU.subtract))
                            av.wait()
                            dve.tensor_scalar(amx, azy, 0.0, None,
                                              ALU.max).then_inc(S["a_m"], 1)
                            dve.tensor_scalar(amn, azy, 0.0, None,
                                              ALU.min).then_inc(S["a_m"], 1)
                        if s == "A_wkv":
                            dve.wait_ge(S["a_v"], 1)
                            dve.wait_ge(S["a_exp"], 1)
                            av(dve.tensor_tensor(ad2v, aP[:, 1, :, :], v_ps, ALU.mult))
                            dve.wait_ge(S["a_exp"], 2)
                            av(dve.tensor_tensor(aQ[:, 0, :, :], aQ[:, 1, :, :], v_ps, ALU.mult))
                            av.wait()
                            for j, add in enumerate((ad2v, aP[:, 1, :, :])):
                                for b in range(BC):
                                    av(dve.tensor_tensor_scan(aAB[:, j, b, 1:T + 1], aQ[:, 2, b, :], add[:, b, :],
                                                              0.0, ALU.mult, ALU.add))
                            av.wait()
                            for j in range(2):
                                av(dve.tensor_tensor(and1[:, j, :, :], aAB[:, j, :, 0:T], aP[:, 0, :, :], ALU.mult))
                            av.wait()
                            av(dve.tensor_tensor(and2[:, :, :, :], and1[:, :, :, :], aQ[:, 0:2, :, :], ALU.add))
                            av.wait()
                            av(dve.reciprocal(ards, and2[:, 1, :, :].rearrange("p b t -> p (b t)")))
                            av.wait()
                            av(dve.tensor_tensor(aw, and2[:, 0, :, :].rearrange("p b t -> p (b t)"), ards,
                                                 ALU.mult))
                            av.wait()
                            dve.wait_ge(S["a_th"], 1)
                            dve.scalar_tensor_tensor(aatt, ath[:, :], 1.0, aw, ALU.add,
                                                     ALU.mult).then_inc(S["a_att"], 1)
                        if s == "A_wo":
                            dve.wait_ge(S["a_wo"], 1)
                            dve.tensor_tensor(ax1[:, :, :], ah[:, :, :], tiles(AB[0]), ALU.add).then_inc(S["a_x1"], 1)
                        if s == "A_ln2":
                            dve.wait_ge(S["a_x1"], 1)
                            stats("a", av, ax1, ast, amv, avar, az, ars, 3)
                        if s == "A_xn2":
                            mix(2, ((axk, FMIXK, "a_xk"), (axr, FMIXR, "a_xr")))
                        if s == "A_out":
                            dve.wait_ge(S["a_th2"], 1)
                            dve.wait_ge(S["a_vk"], 1)
                            av(dve.scalar_tensor_tensor(aq, ath2, 1.0, AB[1][:, :], ALU.add, ALU.mult))
                            av.wait()
                            dve.tensor_tensor(ay0, ax1[:, :, :], aq.rearrange("p (t d) -> p t d", d=D), ALU.add).then_inc(S["a_y"], 1)
                        if s == "B_ln0":
                            dve.wait_ge(S["b_ld"], 16)
                            stats("b", bv_, bx, bst, bmv, bvar, bz, brs, 1)
                        if s == "B_w2":
                            dve.wait_ge(S["b_w2"], 1)
                            dve.wait_ge(S["b_ldm"], 32)
                            bv_(dve.tensor_tensor(by_batch(by[:, :, :]), by_batch(tiles(AB[1])),
                                                  per_batch(bm[:, :, :], by), ALU.mult))
                            bv_.wait()
                            dve.tensor_tensor(bx2[:, :, :], bx[:, :, :], by[:, :, :], ALU.add).then_inc(S["b_x2"], 1)
                        if s == "B_ln1":
                            dve.wait_ge(S["b_x2"], 1)
                            stats("b", bv_, bx2, bst, bmv, bvar, bz, brs, 2)
                        if s == "B_qk":
                            for j, (b_, br_) in enumerate(((col[:, BQ:BQ + 1], bqr), (col[:, BK:BK + 1], bkr))):
                                dve.wait_ge(S["b_q"], 2 * j + 1)
                                if j:
                                    dve.wait_ge(S["b_qk"], 1)
                                dve.scalar_tensor_tensor(apart(bt1), v_ps, b_, every(cos), ALU.add,
                                                         ALU.mult).then_inc(S["b_t"], 1)
                                dve.wait_ge(S["b_q"], 2 * j + 2)
                                dve.scalar_tensor_tensor(apart(bt2), k_ps, br_[:, 0:1], every(sin), ALU.add,
                                                         ALU.mult).then_inc(S["b_t"], 1)
                                dve.wait_ge(S["b_t"], 2 * j + 2)
                                dve.tensor_tensor(bqk[:, j, :], bt1, bt2, ALU.add).then_inc(S["b_qk"], 1)
                            dve.wait_ge(S["b_v"], 1)
                            dve.tensor_tensor(bva[:, :, :, 0:HD],
                                              AB[1][:, 0:NT * 32].rearrange("p (t g v) -> p t g v", t=NT, g=KV),
                                              bv[:, :].rearrange("p (g v) -> p g v", g=KV).unsqueeze(1)
                                              .broadcast_to([P, NT, KV, HD]), ALU.add).then_inc(S["b_va"], 1)
                        if s.startswith("C_s"):
                            u = int(s[3:])
                            bt, hp = divmod(u, H // 2)
                            dve.wait_ge(S["c_s"], u + 1)
                            dve.tensor_reduce(cmx[:, bt, 2 * hp:2 * hp + 2],
                                              CS[u % 2][:, :].rearrange("p (j t) -> p j t", j=2), AX_X, ALU.max,
                                              negate=True).then_inc(S["c_mx"], 1)
                        if s == "C_max":
                            dve.wait_ge(S["c_mx"], 32)
                            dve.tensor_copy(cmp[:, :, 0, :], cmx[:, :, :]).then_inc(S["c_mp"], 1)
                            dve.wait_ge(S["c_mp"], 1)
                            cv(dve.tensor_tensor(cr1[:, :, :], cmx[:, :, :], cmp[:, :, 0, :], ALU.subtract))
                            cv.wait()
                            dve.tensor_copy(cmp[:, :, 1, :], cr1[:, :, :]).then_inc(S["c_mp"], 1)
                            dve.wait_ge(S["c_mp"], 2)
                            cv(dve.tensor_tensor(cr2[:, :, :], cr1[:, :, :], cmp[:, :, 1, :], ALU.subtract))
                            cv.wait()
                            dve.tensor_copy(cmp[:, :, 2, :], cr2[:, :, :]).then_inc(S["c_mp"], 1)
                        if s.startswith("C_o"):
                            o = int(s[3:])
                            b, pp = divmod(o, 2)
                            dve.wait_ge(S["c_ot"], o + 1)
                            t_ = CO[:, :].rearrange("p (j t g v) -> p j t g v", j=2, t=2, g=KV)
                            cv(dve.reciprocal(crs[:, :, :], CO[:, :].rearrange("p (j g v) -> p j g v", j=4, g=KV)[:, :, :, HD]))
                            cv.wait()
                            for j in range(2):
                                ins = dve.tensor_tensor(cctx[:, 2 * b:2 * b + 2, :, pp, j, :], t_[:, j, :, :, 0:HD],
                                                        crs[:, 2 * j:2 * j + 2, :].unsqueeze(3)
                                                        .broadcast_to([P, 2, KV, HD]), ALU.mult)
                                if j:
                                    ins.then_inc(S["c_ctx"], 1)
                        if s == "C_fin":
                            dve.wait_ge(S["c_wo"], 1)
                            dve.wait_ge(S["c_ldm"], 32)
                            cv(dve.tensor_tensor(by_batch(cy), by_batch(tiles(CS[0])),
                                                 per_batch(cm[:, :, :], cy), ALU.mult))
                            cv.wait()
                            dve.tensor_tensor(cxo, cx[:, :, :], cy, ALU.add).then_inc(S["c_y"], 1)
                        if s == "D_ln":
                            dve.wait_ge(S["d_ld"], 16)
                            stats("d", dv, dx, dst, dmv, dvar, dz, drs, 1)
                        if s == "D_router":
                            def over(x_):
                                return x_[:, :].unsqueeze(2).broadcast_to([P, NT, EXPERTS])
                            revb = rev[:, :].unsqueeze(1).broadcast_to([P, NT, EXPERTS])
                            dve.wait_ge(S["d_tp"], 2)
                            dve.tensor_tensor(dlg[:, :, :],
                                              DY[:, 0:NT * EXPERTS].rearrange("p (t e) -> p t e", t=NT),
                                              brt[:, :].unsqueeze(1).broadcast_to([P, NT, EXPERTS]),
                                              ALU.add).then_inc(S["d_lg"], 1)
                            dve.wait_ge(S["d_lg"], 1)

                            def first_max(lg, m_, oh):
                                dv(dve.tensor_reduce(m_[:, :], lg[:, :, :], AX_X, ALU.max))
                                dv.wait()
                                dv(dve.tensor_tensor(deq[:, :, :], lg[:, :, :], over(m_), ALU.is_equal))
                                dv.wait()
                                dv(dve.tensor_tensor(deq[:, :, :], deq[:, :, :], revb, ALU.mult))
                                dv.wait()
                                dv(dve.tensor_reduce(di[:, :], deq[:, :, :], AX_X, ALU.max))
                                dv.wait()
                                dv(dve.tensor_tensor(oh[:, :, :], revb, over(di), ALU.is_equal))
                                dv.wait()
                            first_max(dlg, dm1, doh1)
                            dv(dve.scalar_tensor_tensor(dlg2[:, :, :], doh1[:, :, :], -3e38, dlg[:, :, :],
                                                        ALU.mult, ALU.add))
                            dv.wait()
                            first_max(dlg2, dm2, doh2)
                            dve.tensor_tensor(ddm[:, :], dm2[:, :], dm1[:, :], ALU.subtract).then_inc(S["d_dm"], 1)
                            dve.wait_ge(S["d_e"], 1)
                            dv(dve.tensor_scalar(dp2[:, :], de[:, :], 1.0, None, ALU.add))
                            dv.wait()
                            dv(dve.reciprocal(dp1[:, :], dp2[:, :]))
                            dv.wait()
                            dv(dve.tensor_tensor(dp2[:, :], dp1[:, :], de[:, :], ALU.mult))
                            dv(dve.tensor_tensor(dw1[:, :, :], doh1[:, :, :], over(dp1), ALU.mult))
                            dv.wait()
                            dv(dve.tensor_tensor(doh2[:, :, :], doh2[:, :, :], over(dp2), ALU.mult))
                            dv.wait()
                            dve.tensor_tensor(dwt[:, :, :], dw1[:, :, :], doh2[:, :, :], ALU.add).then_inc(S["d_wt"], 1)
                        if s.startswith("D_q") and int(s[3:]) % FC == FC - 1:
                            e = int(s[3:]) // FC
                            dve.wait_ge(S["d_w2"], FC * (e + 1))
                            dve.wait_ge(S["d_wt"], 1)
                            if e:
                                dve.wait_ge(S["d_acc"], NT * e)
                            for t in range(NT):
                                y_ = DY[:, t * P:(t + 1) * P]
                                if e == 0:
                                    ins = dve.tensor_scalar(dacc[:, t, :], y_, dwt[:, t, e:e + 1], None, ALU.mult)
                                else:
                                    ins = dve.scalar_tensor_tensor(dacc[:, t, :], y_, dwt[:, t, e:e + 1],
                                                                   dacc[:, t, :], ALU.mult, ALU.add)
                                ins.then_inc(S["d_acc"], 1)
                            if e == EXPERTS - 1:
                                dve.wait_ge(S["d_acc"], NT * EXPERTS)
                                dve.wait_ge(S["d_ldm"], 32)
                                dv(dve.tensor_tensor(by_batch(dy), by_batch(dacc[:, :, :]),
                                                     per_batch(dm[:, :, :], dy), ALU.mult))
                                dv.wait()
                                dve.tensor_tensor(dxo, dx[:, :, :], dy, ALU.add)\
                                    .then_inc(S["d_out"], 1)

            new_round()

        for n in range(STAGES - 1):
            one_round(n, [n >= s for s in range(STAGES)])
        with nc.Fori(STAGES - 1, CHUNKS) as n:
            one_round(n, [True] * STAGES)
        for n in range(CHUNKS, CHUNKS + STAGES - 1):
            one_round(n, [n - s < CHUNKS for s in range(STAGES)])


ROWS_DONE = 4 + 4 + 2 + 2 * (4 + 2 * 4) + 6


def schedule():
    out, q, u = [], 0, 0

    def fill(units, quanta):
        nonlocal q, u
        for k in range(max(units, quanta)):
            if k < quanta and q < EXPERTS * FC:
                out.append(f"D_q{q}")
                q += 1
            if k < units and u < 32:
                out.append(f"C_s{u}")
                u += 1

    out += ["D_ln", "A_ln0", "D_router", "A_ln1"]
    fill(0, 1)
    out += ["A_xn"]
    fill(0, 1)
    out += ["A_rkv"]
    fill(4, 2)
    out += ["A_wkv"]
    fill(4, 3)
    out += ["A_wo"]
    fill(1, 1)
    out += ["A_ln2"]
    fill(2, 1)
    out += ["A_xn2"]
    fill(2, 1)
    out += ["A_fk", "A_fr"]
    fill(3, 2)
    out += ["A_vk"]
    fill(2, 1)
    out += ["A_out", "B_ln0"]
    fill(2, 1)
    out += ["B_h", "B_w1"]
    fill(4, 2)
    out += ["B_w2"]
    fill(2, 1)
    out += ["B_ln1"]
    fill(2, 1)
    out += ["B_h2"]
    fill(2, 1)
    out += ["B_qk"]
    fill(4, 2)
    out += ["B_split", "C_max"]
    fill(0, 3)
    for g in range(8):
        out.append(f"C_g{g}")
        fill(0, 1)
        if g % 2 == 0 and g >= 2:
            out.append(f"C_o{(g - 2) // 2}")
    out += ["C_o3", "C_fin"]
    fill(0, 32)
    return out


SCHEDULE = schedule()


def kernel(**inputs):
    import ml_dtypes
    import concourse.bacc as _bacc
    from concourse import mybir as _mybir
    from concourse.bass_utils import run_bass_kernel_spmd as _run

    i = {k: np.ascontiguousarray(v) for k, v in inputs.items()}
    bf16 = ml_dtypes.bfloat16
    inv = (1.0 / 10000.0 ** (np.arange(0, HD, 2, dtype=np.float32) / HD)).astype(np.float32)
    ang = (np.arange(T, dtype=np.float32)[:, None] * inv[None, :]).astype(np.float32)
    by_row = [(p % HD) % (HD // 2) for p in range(P)]
    cos = np.ascontiguousarray(np.cos(ang).T[by_row])
    sin = np.ascontiguousarray(np.sin(ang).T[by_row])
    rot = np.zeros((P, P), np.float32)
    for h in range(H):
        for r in range(HD // 2):
            rot[h * HD + 2 * r + 1, h * HD + r] = -1.0
            rot[h * HD + 2 * r, h * HD + HD // 2 + r] = 1.0
    rotk = np.tile(rot[0:KV * HD, 0:KV * HD], (1, P // (KV * HD)))
    arrays = {k: v for k, v in i.items() if k in _PLAIN}
    arrays["x"] = i["L0_attn_x"].reshape(B * T, D)
    arrays["L1_attn_bv"] = i["L1_attn_bv"]
    arrays.update({
        "c_ident": np.eye(P, dtype=np.float32), "c_identb": np.eye(P).astype(bf16), "c_cos": cos, "c_sin": sin,
        "c_rotq": rot, "c_rotk": np.ascontiguousarray(rotk),
        "c_rev": np.tile(np.arange(EXPERTS, 0, -1, dtype=np.float32), (P, 1)),
        "c_ones3": np.ones((PARTS, P), bf16), "c_mask3": np.eye(PARTS, dtype=np.float32),
        "c_onesk": np.ones((PARTS, KV * N), bf16),
    })
    c = [i["L0_attn_" + k].reshape(D) for k in
         ("ln1_w", "ln1_b", "ln2_w", "ln2_b", "time_decay", "time_first", "time_mix_k", "time_mix_v", "time_mix_r",
          "f_time_mix_k", "f_time_mix_r")]
    c += [i["L1_attn_bq"], np.tile(i["L1_attn_bk"], P // (KV * HD))]
    c += list(i["L0_ffn_b1"].reshape(FC, P))
    arrays["cols"] = np.ascontiguousarray(np.stack(c, axis=1))
    arrays["wqT"] = np.ascontiguousarray(i["L1_attn_Wq"].T)
    arrays["wkT"] = np.ascontiguousarray(np.tile(i["L1_attn_Wk"].T, (1, P // (KV * HD))))
    arrays["wvT"] = np.ascontiguousarray(i["L1_attn_Wv"].T)
    arrays["woT"] = np.ascontiguousarray(i["L1_attn_Wo"].T)
    arrays["e1b"] = np.ascontiguousarray(i["L1_ffn_b1"].reshape(EXPERTS * FC, P).T)
    arrays["cT0"] = np.ascontiguousarray(i["L0_c"].T)
    arrays["cT1"] = np.ascontiguousarray(i["L1_c"].T)
    arrays["brow"] = np.concatenate([i["L1_ffn_b2"].reshape(-1), i["L1_attn_bo"], i["L0_ffn_b2"]])
    nc = _bacc.Bacc("TRN2", target_bir_lowering=False, num_devices=1)
    aps, feeds = {}, {}
    for name, v in arrays.items():
        feeds["in_" + name] = v
        aps[name] = nc.dram_tensor("in_" + name, v.shape, _mybir.dt.from_np(v.dtype), kind="ExternalInput").ap()
    aps["out"] = nc.dram_tensor("out_0_dram", (B * T, D), _mybir.dt.float32, kind="ExternalOutput").ap()
    program(nc, aps)
    r = _run(nc, [feeds], core_ids=[0])
    return r.results[0]["out_0_dram"].reshape(B, T, D)


_PLAIN = ["L0_attn_w_key", "L0_attn_w_value", "L0_attn_w_recept", "L0_attn_w_output", "L0_attn_f_w_key",
          "L0_attn_f_w_recept", "L0_attn_f_w_value", "L0_ffn_W1", "L0_ffn_W2", "L0_wmod", "L1_wmod", "L1_attn_Wq",
          "L1_attn_Wk", "L1_attn_bv", "L1_ffn_W_router", "L1_ffn_b_router", "L1_ffn_W1", "L1_ffn_W2"]
```

```python
from contextlib import ExitStack

import numpy as np

import concourse.bass as bass
from concourse import mybir

F32 = mybir.dt.float32
BF16 = mybir.dt.bfloat16
I32 = mybir.dt.int32
U32 = mybir.dt.uint32
ALU = mybir.AluOpType
ACT = mybir.ActivationFunctionType
AX_X = mybir.AxisListType.X

P = 128
D = 128
B, T = 32, 256
BC = 2
N = BC * T
NT = N // P
CHUNKS = B // BC
FC = 4
H, KV, HD = 16, 4, 8
G = H // KV
EXPERTS = 8
PARTS = 3
SROWS = PARTS * PARTS * HD
KROWS = SROWS + PARTS
EPS = 1e-5
NEG_INIT = -1e30
SCALE = float(HD) ** -0.5
GROUP = 4
GROUPS = CHUNKS // GROUP
GT = GROUP * NT
SLOT_TILES = 2 * GT + EXPERTS
MT = SLOT_TILES // GROUP
MW = 2
WROW = FC * P + FC + FC * D
STAGES = 5
FIRST_SORT = GROUP + STAGES - 1
FIRST_TILES = FIRST_SORT + 1
FIRST_SUM = FIRST_TILES + GROUP
ROUNDS = CHUNKS + FIRST_SUM

(LN1W, LN1B, LN2W, LN2B, DECAY, FIRST, MIXK, MIXV, MIXR, FMIXK, FMIXR, BQ, BK, BKN,
 L0B1) = range(15)
NCOL = L0B1 + FC
CB0, SB0, CA1, SA1 = range(4)
MODC = 4
OH1, OH2, WT, P1, P2 = 0, EXPERTS, 2 * EXPERTS, 3 * EXPERTS, 3 * EXPERTS + 1
INFO = 3 * EXPERTS + 2
SA, CA, GA, SB, CB, GB = range(6)

EVENTS = """
a_ld a_ldm a_var a_rstd a_norm a_h0 a_h a_tp a_xn a_dx a_xk a_xv a_xr a_r a_th a_k a_v a_m a_exp a_att a_wo
a_x1 a_fk a_rl a_sq a_fr a_th2 a_vk a_y a_st a_vec a_scl a_pol
b_ld b_ldm b_var b_rstd b_norm b_tp b_h b_w1 b_hs b_w2 b_x2 b_st b_q b_t b_v b_va b_qk b_p b_r b_st2 b_vec
c_ldq c_ldv c_ldm c_s c_mx c_mp c_mt c_mT c_rows c_s2 c_p c_pv c_o c_ot c_ctx c_ct c_cT c_wo c_y c_st c_vec
r_ld r_ldm r_var r_rstd r_norm r_h0 r_hn r_tp r_h r_rt r_lg r_dm r_e r_info r_st r_vec
s_zero s_ld s_tot s_pre s_slot s_tile s_st s_ldx0 s_ldx1 s_vec
m_ldx m_lde m_w0 m_w1 m_tp m_x m_h m_r m_y m_o m_st
k_ldi k_lds k_ldx k_tp k_wT k_b k_out k_st k_vec
""".split()


KEPT = "s_sc0 s_sc1 k_g".split()


class Count:

    def __init__(self, eng, sem):
        self.eng, self.sem, self.n = eng, sem, 0

    def __call__(self, ins):
        ins.then_inc(self.sem, 1)
        self.n += 1
        return self.n

    def wait(self, n=None):
        self.eng.wait_ge(self.sem, self.n if n is None else n)


def program(nc, a):
    ctx = ExitStack()
    with ctx:
        def sb(name, shape, dt=F32):
            return ctx.enter_context(nc.sbuf_tensor(name, shape, dt))

        def scratch(name, shape, dt=F32):
            return nc.dram_tensor(name, shape, dt).ap()

        bank = [ctx.enter_context(nc.psum_tensor(f"bank{n}", [P, 512], F32)) for n in range(8)]
        AB, BB, CS, CO, DB, MB = bank[0:2], bank[2], bank[3:5], bank[5], bank[6], bank[7]

        x_a = scratch("x_a", [B * T, D])
        x_b = scratch("x_b", [B * T, D])
        x_c = scratch("x_c", [B * T, D])
        q_parts = scratch("q_parts", [CHUNKS * PARTS * P, N], BF16)
        k_parts = scratch("k_parts", [CHUNKS * PARTS * P, N], BF16)
        v_tiles = scratch("v_tiles", [CHUNKS * P, NT * KV * 32])
        rows0 = scratch("rows0", [B, 6 * D])
        rows1 = scratch("rows1", [B, 6 * D])
        cols_mod = scratch("cols_mod", [P, B * MODC])
        x_h = scratch("x_h", [B * T, D])
        info_d = scratch("info_d", [CHUNKS * P, NT * INFO])
        slot_d = scratch("slot_d", [CHUNKS * P, 2 * NT], U32)
        tile_d = [scratch(f"tile_d{g}", [1, SLOT_TILES], I32) for g in range(GROUPS)]
        x_slots = [scratch(f"x_slots{g}", [SLOT_TILES * P, D]) for g in range(GROUPS)]
        y_slots = [scratch(f"y_slots{g}", [SLOT_TILES * P, D]) for g in range(GROUPS)]

        ident = sb("ident", [P, P])
        identb = sb("identb", [P, P], BF16)
        cos = sb("cos", [P, T])
        sin = sb("sin", [P, T])
        col = sb("col", [P, NCOL])
        negw = sb("negw", [P, 1])
        half = sb("half", [P, NT])
        wk, wv, wr, wo = (sb(n, [P, D]) for n in ("wk", "wv", "wr", "wo"))
        fwk = sb("fwk", [P, FC * P])
        fwr = sb("fwr", [P, D])
        fwv = sb("fwv", [P, FC, D])
        w1 = sb("w1", [P, FC * P])
        w2 = sb("w2", [P, FC, D])
        wqT, wqrT, wkT, wkrT = (sb(n, [P, P]) for n in ("wqT", "wqrT", "wkT", "wkrT"))
        bqr = sb("bqr", [P, 1])
        bkr = sb("bkr", [P, 1])
        wvT = sb("wvT", [P, KV * HD])
        woT = sb("woT", [P, D])
        bv = sb("bv", [P, KV * HD])
        wrt = sb("wrt", [P, EXPERTS])
        brt = sb("brt", [P, EXPERTS])
        rev = sb("rev", [P, EXPERTS])
        eb2 = sb("eb2", [EXPERTS, D])
        upper = sb("upper", [P, P])
        onesf = sb("onesf", [P, P])
        restart = sb("restart", [P, EXPERTS * GT])
        steps16 = sb("steps16", [P, GT])
        steps1 = sb("steps1", [P, SLOT_TILES])
        ones3 = sb("ones3", [PARTS, P], BF16)
        brow = sb("brow", [PARTS, 2 * D], BF16)
        BO, B2 = 0, 1

        ax = sb("ax", [P, NT, D])
        am = sb("am", [P, BC, 3, D])
        ast = sb("ast", [P, NT, 6])
        amv = sb("amv", [P, NT, 2])
        avar = sb("avar", [P, NT])
        ars = sb("ars", [P, NT])
        az = sb("az", [P, NT, D])
        ah0 = sb("ah0", [P, NT, D])
        ah = sb("ah", [P, NT, D])
        axn = sb("axn", [P, BC, T + 1])
        adx = sb("adx", [P, BC, T])
        axk, axv, axr = (sb(n, [P, BC, T]) for n in ("axk", "axv", "axr"))
        ath = sb("ath", [P, N])
        aE = sb("aE", [P, BC, T + 1])
        wkv = sb("wkv", [P, 2 * FC, N])
        arl, asq = wkv[:, 0:FC, :], wkv[:, FC:2 * FC, :]
        azy, amx, amn, aP = (wkv[:, 2 * k:2 * k + 2, :].rearrange("p s (b t) -> p s b t", b=BC) for k in range(4))
        ards, aatt = wkv[:, 0, :], wkv[:, 1, :]
        aQ = sb("aQ", [P, 3, BC, T])
        ad2v = wkv[:, 2, :].rearrange("p (b t) -> p b t", b=BC)
        aAB = sb("aAB", [P, 2, BC, T + 1])
        and1 = sb("and1", [P, 2, BC, T])
        and2 = sb("and2", [P, 2, BC, T])
        aw = adx[:, :, :].rearrange("p b t -> p (b t)")
        ax1 = ah0
        ath2, aq = (aQ[:, k, :, :].rearrange("p b t -> p (b t)") for k in range(2))
        ay0, ay1, axo = (w_.rearrange("p b (t d) -> p (b t) d", d=D) for w_ in
                         (aQ[:, 2, :, :], and1[:, 0, :, :], and1[:, 1, :, :]))

        bx = sb("bx", [P, NT, D])
        bm = sb("bm", [P, BC, D])
        bc = sb("bc", [P, BC, MODC])
        bst = sb("bst", [P, NT, 6])
        bmv = sb("bmv", [P, NT, 2])
        bvar = sb("bvar", [P, NT])
        brs = sb("brs", [P, NT])
        bz = sb("bz", [P, NT, D])
        bh = sb("bh", [P, N])
        bhs = sb("bhs", [P, FC, N])
        by = bz
        bx2 = sb("bx2", [P, NT, D])
        bt1, bt2, br1, br2 = bhs[:, 0, :], bhs[:, 1, :], bhs[:, 2:4, :], bhs[:, 0:2, :]
        bqk = sb("bqk", [P, 2, N])
        bp = sb("bp", [P, PARTS, 2, N], BF16)
        bva = sb("bva", [P, NT, KV, 32])

        cQ = sb("cQ", [P, H, N], BF16)
        cK = sb("cK", [P, KV, N], BF16)
        cV = sb("cV", [P, NT, KV, 32])
        cx = sb("cx", [P, NT, D])
        cm = sb("cm", [P, BC, D])
        cmx = sb("cmx", [P, NT, H])
        cmp = sb("cmp", [P, NT, PARTS, H], BF16)
        cr1 = sb("cr1", [P, NT, H])
        cr2 = sb("cr2", [P, NT, H])
        cmT = sb("cmT", [PARTS * H, N], BF16)
        cP = sb("cP", [P, 8, N])
        cos_ = sb("cos_", [P, N])
        crs = sb("crs", [P, 4, KV])
        cctx = sb("cctx", [P, NT, KV, 2, 2, HD])
        ccT = sb("ccT", [P, N])
        cy, cxo = (cP[:, k, :].rearrange("p (t d) -> p t d", d=D) for k in range(2))

        rx = sb("rx", [P, NT, D])
        rm = sb("rm", [P, BC, 2, D])
        rst = sb("rst", [P, NT, 6])
        rmv = sb("rmv", [P, NT, 2])
        rvar = sb("rvar", [P, NT])
        rrs = sb("rrs", [P, NT])
        rz = sb("rz", [P, NT, D])
        rh0 = rx
        rhn = sb("rhn", [P, NT, D])
        rh = sb("rh", [P, N])
        rinfo = sb("rinfo", [P, NT, INFO])
        rlg, req, rlg2, rw1, rw2 = (sb(n, [P, NT, EXPERTS]) for n in ("rlg", "req", "rlg2", "rw1", "rw2"))
        rm1, rm2, ri, rdm, re, rp = (sb(n, [P, NT]) for n in ("rm1", "rm2", "ri", "rdm", "re", "rp"))

        sinfo = sb("sinfo", [P, GROUP, NT * INFO])
        scnt, sinc, spos = (sb(n, [P, EXPERTS, GT]) for n in ("scnt", "sinc", "spos"))
        sprod = sb("sprod", [P, GT, EXPERTS])
        stot, snum, snt, sti, sbase, sone = (sb(n, [P, EXPERTS]) for n in ("stot", "snum", "snt", "sti", "sbase", "sone"))
        scmp = scnt
        scm2 = sb("scm2", [P, SLOT_TILES, EXPERTS])
        sslf = sb("sslf", [P, 2, GT])
        sslot = sb("sslot", [P, GROUP, 2, NT], U32)
        sef = sb("sef", [P, SLOT_TILES])
        sei = sb("sei", [P, SLOT_TILES], I32)
        sx = sb("sx", [P, 2, NT, D])

        mX = sb("mX", [P, MT, D])
        mE = sb("mE", [1, MT], I32)
        mW = sb("mW", [P, MW, WROW])
        mT = sb("mT", [P, MT * P])
        mH = sb("mH", [P, FC * P])
        mY = mX

        kinfo = sb("kinfo", [P, NT, INFO])
        kslot = sb("kslot", [P, 2, NT], U32)
        kx = sb("kx", [P, NT, D])
        km = sb("km", [P, BC, D])
        kg = sb("kg", [P, 2, NT, D])
        kwT = sb("kwT", [EXPERTS, N])
        kacc = kg[:, 0, :, :]

        sems = [ctx.enter_context(nc.semaphore(n)) for n in EVENTS]
        S = dict(zip(EVENTS, sems))
        span = range(sems[0].num, sems[-1].num + 1)
        assert len(span) == len(sems)

        S.update((n, ctx.enter_context(nc.semaphore(n))) for n in KEPT)

        def new_round():
            nc.all_engine_barrier()
            nc.gpsimd.sem_clear(span)
            nc.all_engine_barrier()

        def tiles(ap):
            return ap[:, :].rearrange("p (t d) -> p t d", t=NT)

        def per_batch(rows, like):
            return rows.unsqueeze(2).broadcast_to([P, BC, NT // BC, D])

        def by_batch(ap):
            return ap.rearrange("p (b t) d -> p b t d", b=BC)

        with nc.Block() as block:
            L, M, V2, V3, PW = S["a_ld"], S["a_ldm"], S["a_vec"], S["a_scl"], S["a_pol"]
            mm = S["a_k"]
            tc0 = arl[:, 0, 0:B]
            tc1 = arl[:, 0, B:2 * B]
            ec = arl[:, 0, 2 * B:4 * B]
            sc = arl[:, 0, 4 * B:6 * B]
            wmod0, wmod1 = asq[:, 0:2, :].rearrange("p a b -> p (a b)")[:, 0:6 * D], \
                asq[:, 2:4, :].rearrange("p a b -> p (a b)")[:, 0:6 * D]
            wq_n, wk_n = az[:, 0, :], az[0:KV * HD, 1, :]
            rq, rk = az[:, 2, :], az[0:KV * HD, 3, :]
            rowbuf = [cP[0:B, 0:2, :].rearrange("p a b -> p (a b)")[:, 0:6 * D],
                      cP[0:B, 2:4, :].rearrange("p a b -> p (a b)")[:, 0:6 * D]]
            rowneg = cP[0:B, 4, :]
            rowsgn = cP[0:B, 5, :]
            colbuf = cP[:, 6, 0:B * MODC].rearrange("p (b s) -> p b s", s=MODC)
            NB = 2 * D
            braw = arl[0:PARTS, 1:4, :].rearrange("p a b -> p (a b)")[:, 0:NB]
            br_1 = bhs[0:PARTS, 0:3, :].rearrange("p a b -> p (a b)")[:, 0:NB]
            br_2 = bqk[0:PARTS, 0, 0:NB]
            bpart = cQ[0:PARTS, 0:9, :].rearrange("p a b -> p (a b)")[:, 0:PARTS * NB] \
                .rearrange("p (s n) -> p s n", s=PARTS)
            mask3 = ax[0:PARTS, 0, 0:PARTS]
            bsum = [bhs[0:PARTS, 0:3, :].rearrange("p a b -> p (a b)")[:, 0:NB],
                    bqk[0:PARTS, 1, 0:NB]]
            loads = [
                (ident[:, :], a["c_ident"]), (identb[:, :], a["c_identb"]), (cos[:, :], a["c_cos"]),
                (sin[:, :], a["c_sin"]), (col[:, :], a["cols"]), (wk[:, :], a["L0_attn_w_key"]),
                (wv[:, :], a["L0_attn_w_value"]), (wr[:, :], a["L0_attn_w_recept"]),
                (wo[:, :], a["L0_attn_w_output"]), (fwk[:, :], a["L0_attn_f_w_key"]),
                (fwr[:, :], a["L0_attn_f_w_recept"]),
                (fwv[:, :, :], a["L0_attn_f_w_value"].rearrange("(c p) d -> p c d", p=P)),
                (w1[:, :], a["L0_ffn_W1"]),
                (w2[:, :, :], a["L0_ffn_W2"].rearrange("(c p) d -> p c d", p=P)),
                (wqT[:, :], a["wqT"]), (wkT[:, :], a["wkT"]), (wvT[:, :], a["wvT"]), (woT[:, :], a["woT"]),
                (wq_n, a["wq_n"]), (wk_n, a["L1_attn_Wk"]), (rq, a["c_rotq"]), (rk, a["c_rotk"]),
                (bv[:, :], a["L1_attn_bv"].partition_broadcast(P)),
                (wrt[:, :], a["L1_ffn_W_router"]), (brt[:, :], a["L1_ffn_b_router"].partition_broadcast(P)),
                (rev[:, :], a["c_rev"]), (eb2[:, :], a["L1_ffn_b2"]), (upper[:, :], a["c_upper"]),
                (restart[:, :], a["c_restart"]), (steps16[:, :], a["c_steps16"]), (steps1[:, :], a["c_steps1"]),
                (ones3[:, :], a["c_ones3"]), (mask3, a["c_mask3"]),
                (cK[SROWS:KROWS, :, :].rearrange("p g n -> p (g n)"), a["c_onesk"]),
                (tc0, a["cT0"]), (tc1, a["cT1"]), (wmod0, a["L0_wmod"]), (wmod1, a["L1_wmod"]),
                (braw, a["brow"].partition_broadcast(PARTS)),
            ]

            @block.sync
            def _(sp):
                for dst_, src_ in loads:
                    sp.dma_start(dst_, src_).then_inc(L, 16)
                sp.wait_ge(V2, ROWS_DONE)
                sp.dma_start(rows0, rowbuf[0]).then_inc(M, 16)
                sp.dma_start(rows1, rowbuf[1]).then_inc(M, 16)
                sp.dma_start(cols_mod, cP[:, 6, 0:B * MODC]).then_inc(M, 16)
                sp.wait_ge(M, 48)

            ALL = 16 * len(loads)

            @block.gpsimd
            def _(pool):
                pool.memset(half[:, :], -0.5)
                pool.memset(onesf[:, :], 1.0)
                pool.memset(sone[:, :], 1.0)
                pool.memset(mH[:, :], 0.0)
                pool.memset(axn[:, :, 0:1], 0.0)
                pool.memset(aE[:, :, 0:1], NEG_INIT)
                pool.memset(aAB[:, :, :, 0:1].rearrange("p a b o -> p (a b) o"), 0.0)
                pool.memset(bva[:, :, :, :].rearrange("p t g v -> p (t g v)"), 0.0).then_inc(PW, 1)
                pool.wait_ge(PW, 1)
                pool.memset(bva[:, :, :, 8:9].rearrange("p t g v -> p (t g) v"), 1.0).then_inc(PW, 1)

            @block.scalar
            def _(act):
                act.wait_ge(L, ALL)
                act.activation(negw[:, :], col[:, DECAY:DECAY + 1], ACT.Exp).then_inc(V3, 1)
                act.activation(ec, arl[:, 0, 0:2 * B], ACT.Exp, scale=-1.0).then_inc(V3, 1)

            @block.tensor
            def _(pe):
                pe.wait_ge(L, ALL)
                pe.matmul(bank[0][:, 0:P], wq_n, rq, start=True, stop=True)
                pe.matmul(bank[1][:, 0:P], wk_n, rk, start=True, stop=True)
                pe.matmul(bank[2][:, 0:1], rq, col[:, BQ:BQ + 1], start=True, stop=True)
                pe.matmul(bank[3][:, 0:1], rk, col[0:KV * HD, BKN:BKN + 1], start=True, stop=True).then_inc(mm, 1)
                pe.wait_ge(V2, 4)
                for l, wm in enumerate((wmod0, wmod1)):
                    s = sc[:, l * B:(l + 1) * B]
                    pe.matmul(bank[4 + 2 * l][0:B, 0:3 * D], s, wm[:, 0:3 * D], start=True, stop=True)
                    pe.matmul(bank[5 + 2 * l][0:B, 0:3 * D], s, wm[:, 3 * D:6 * D], start=True,
                              stop=True).then_inc(mm, 1)
                pe.wait_ge(V2, 8)
                for j, (l, kind) in enumerate(((0, CB), (0, SB), (1, CA), (1, SA))):
                    wm = (wmod0, wmod1)[l]
                    pe.matmul(bank[0][:, j * 128:j * 128 + B], wm[:, kind * D:(kind + 1) * D],
                              sc[:, l * B:(l + 1) * B], start=True, stop=True).then_inc(mm, 1)

            @block.vector
            def _(dve):
                c = Count(dve, V2)
                dve.wait_ge(L, ALL)
                dve.wait_ge(V3, 2)
                c(dve.tensor_scalar(negw[:, :], negw[:, :], -1.0, None, ALU.mult))
                c(dve.tensor_scalar(ec, ec, 1.0, None, ALU.add))
                c.wait()
                c(dve.reciprocal(ec, ec))
                c.wait()
                c(dve.tensor_tensor(sc, arl[:, 0, 0:2 * B], ec, ALU.mult))
                dve.wait_ge(mm, 1)
                c(dve.tensor_copy(wqrT[:, :], bank[0][:, 0:P]))
                c(dve.tensor_copy(wkrT[:, :], bank[1][:, 0:P]))
                c(dve.tensor_copy(bqr[:, :], bank[2][:, 0:1]))
                c(dve.tensor_copy(bkr[:, :], bank[3][:, 0:1]))
                c(dve.tensor_scalar(wo[:, :], wo[:, :], 0.5, None, ALU.mult))
                c(dve.tensor_scalar(fwv[:, :, :], fwv[:, :, :], 0.5, None, ALU.mult))
                for l in range(2):
                    dve.wait_ge(mm, 2 + l)
                    rb = rowbuf[l]
                    for j in range(6):
                        src_ = bank[4 + 2 * l + j // 3][0:B, (j % 3) * D:(j % 3 + 1) * D]
                        out_ = rb[:, j * D:(j + 1) * D]
                        if j in (SA, SB):
                            c(dve.tensor_copy(out_, src_))
                        elif j in (CA, CB):
                            c(dve.tensor_scalar(out_, src_, 1.0, None, ALU.add))
                        else:
                            c(dve.tensor_scalar(rowneg[:, 0:D], src_, -1.0, 0.25, ALU.mult, ALU.max))
                            c(dve.tensor_scalar(rowsgn[:, 0:D], src_, 0.0, 2.0, ALU.is_ge, ALU.mult))
                            c.wait()
                            c(dve.tensor_tensor(rowneg[:, 0:D], src_, rowneg[:, 0:D], ALU.max))
                            c.wait()
                            c(dve.scalar_tensor_tensor(out_, rowsgn[:, 0:D], -1.0, rowneg[:, 0:D],
                                                       ALU.add, ALU.mult))
                            c.wait()
                dve.wait_ge(mm, 3 + MODC)
                for j in range(MODC):
                    src_ = bank[0][:, j * 128:j * 128 + B]
                    c(dve.tensor_scalar(colbuf[:, :, j], src_, 0.0 if j % 2 else 1.0, None, ALU.add))
                assert c.n == ROWS_DONE, c.n
                c(dve.tensor_copy(bpart[:, 0, :], braw))
                c.wait()
                c(dve.tensor_tensor(br_1, braw, bpart[:, 0, :], ALU.subtract))
                c.wait()
                c(dve.tensor_copy(bpart[:, 1, :], br_1))
                c.wait()
                c(dve.tensor_tensor(br_2, br_1, bpart[:, 1, :], ALU.subtract))
                c.wait()
                c(dve.tensor_copy(bpart[:, 2, :], br_2))
                c.wait()
                c(dve.tensor_scalar(bsum[0], bpart[:, 0, :], mask3[:, 0:1], None, ALU.mult))
                c.wait()
                c(dve.scalar_tensor_tensor(bsum[1], bpart[:, 1, :], mask3[:, 1:2], bsum[0], ALU.mult, ALU.add))
                c.wait()
                c(dve.scalar_tensor_tensor(brow[:, :], bpart[:, 2, :], mask3[:, 2:3], bsum[1], ALU.mult, ALU.add))
                c.wait()

        new_round()

        def one_round(n, live):
            order = {e: [s for s in o if s[0] in live] for e, o in SCHEDULE.items()}
            ca, cb, cc, cg, cr, ck = n, n - 1, n - 2, n - 3, n - 4, n - FIRST_SUM
            gs, gm, gk = (live.get(k) for k in "SMK")
            on = {k: k in live for k in "ABCGRSMK"}

            def rows(dram, i):
                return dram[bass.ds(i * N, N), :].rearrange("(t p) d -> p t d", p=P)

            def row_mod(dram, i, k0, k):
                return dram[bass.ds(i * BC, BC), k0 * D:(k0 + k) * D].partition_broadcast(P)

            def load_sorted(sp, c):
                sp.dma_start(sx[:, c % 2, :, :], rows(x_h, gs * GROUP + c)).then_inc(S[f"s_ldx{c % 2}"], 16)

            def load_weights(sp, t):
                row = sp.value_load(mE[0:1, t:t + 1], min_val=0, max_val=(EXPERTS - 1) * P)
                sp.dma_start(mW[:, t % MW, :], a["wexp"][bass.ds(row, P), :]).then_inc(S[f"m_w{t % MW}"], 16)

            with nc.Block() as block:
                @block.sync
                def _(sp):
                    if on["M"]:
                        first = (n - FIRST_TILES - GROUP * gm) * MT
                    for g in live.get("Z", ()):
                        sp.dma_start(x_slots[g].rearrange("(p t) d -> p (t d)", p=P)
                                     .rearrange("p (t w) -> p t w", w=FC * P),
                                     mH[:, :].unsqueeze(1).broadcast_to([P, SLOT_TILES // FC, FC * P])
                                     ).then_inc(S["s_zero"], 16)
                    for s in order["SP"]:
                        if s == "A_ld":
                            sp.dma_start(ax[:, :, :], rows(a["x"], ca)).then_inc(S["a_ld"], 16)
                        if s == "A_ldm":
                            sp.dma_start(am[:, :, :, :].rearrange("p b s d -> p b (s d)"),
                                         row_mod(rows0, ca, SA, 3)).then_inc(S["a_ldm"], 16)
                        if s == "B_ld":
                            sp.dma_start(bx[:, :, :], rows(x_a, cb)).then_inc(S["b_ld"], 16)
                        if s == "B_ldm":
                            sp.dma_start(bc[:, :, :].rearrange("p b s -> p (b s)"),
                                         cols_mod[:, bass.ds(cb * BC * MODC, BC * MODC)]).then_inc(S["b_ldm"], 16)
                            sp.dma_start(bm[:, :, :], row_mod(rows0, cb, GB, 1)).then_inc(S["b_ldm"], 16)
                        if s == "C_ldq":
                            if on["G"]:
                                sp.wait_ge(S["c_s2"], 32)
                            for i in range(PARTS):
                                r0 = i * PARTS * HD
                                sp.dma_start(cQ[r0:r0 + PARTS * HD, :, :].rearrange("r h t -> r (h t)"),
                                             q_parts[bass.ds((cc * PARTS + i) * P, P), :]
                                             .rearrange("(d h) t -> d (h t)", d=HD).unsqueeze(0)
                                             .broadcast_to([PARTS, HD, H * N])).then_inc(S["c_ldq"], 16)
                                sp.dma_start(cK[r0:r0 + PARTS * HD, :, :],
                                             k_parts[bass.ds(cc * PARTS * P, PARTS * P), :]
                                             .rearrange("(r g k) t -> r g k t", g=KV, k=G)[:, :, 0, :]
                                             ).then_inc(S["c_ldq"], 16)
                        if s == "G_ldv":
                            sp.dma_start(cV[:, :, :, :].rearrange("p t g v -> p (t g v)"),
                                         v_tiles[bass.ds(cg * P, P), :]).then_inc(S["c_ldv"], 16)
                        if s == "G_ldm":
                            sp.dma_start(cx[:, :, :], rows(x_b, cg)).then_inc(S["c_ldm"], 16)
                            sp.dma_start(cm[:, :, :], row_mod(rows1, cg, GA, 1)).then_inc(S["c_ldm"], 16)
                        if s == "R_ld":
                            sp.dma_start(rx[:, :, :], rows(x_c, cr)).then_inc(S["r_ld"], 16)
                        if s == "R_ldm":
                            sp.dma_start(rm[:, :, :, :].rearrange("p b s d -> p b (s d)"),
                                         row_mod(rows1, cr, SB, 2)).then_inc(S["r_ldm"], 16)
                        if s == "S_ld":
                            sp.dma_start(sinfo[:, :, :], info_d[gs * GROUP * P:(gs + 1) * GROUP * P, :]
                                         .rearrange("(c p) i -> p c i", p=P)).then_inc(S["s_ld"], 16)
                            for c in range(2):
                                load_sorted(sp, c)
                        if s == "M_lde":
                            sp.dma_start(mE[:, :], tile_d[gm][:, bass.ds(first, MT)]).then_inc(S["m_lde"], 16)
                        if s == "M_ldx":
                            sp.dma_start(mX[:, :, :], x_slots[gm][bass.ds(first * P, MT * P), :]
                                         .rearrange("(t p) d -> p t d", p=P)).then_inc(S["m_ldx"], 16)
                        if s == "M_ldw":
                            sp.wait_ge(S["m_lde"], 16)
                            for t in range(MW):
                                load_weights(sp, t)
                        if s == "K_lds":
                            sp.dma_start(kslot[:, :, :].rearrange("p k t -> p (k t)"),
                                         slot_d[bass.ds(ck * P, P), :]).then_inc(S["k_lds"], 16)
                        if s == "K_ldi":
                            sp.dma_start(kinfo[:, :, :].rearrange("p t i -> p (t i)"),
                                         info_d[bass.ds(ck * P, P), :]).then_inc(S["k_ldi"], 16)
                        if s == "K_ldx":
                            sp.dma_start(kx[:, :, :], rows(x_c, ck)).then_inc(S["k_ldx"], 16)
                            sp.dma_start(km[:, :, :], row_mod(rows1, ck, GB, 1)).then_inc(S["k_ldx"], 16)
                        if s == "A_out":
                            sp.wait_ge(S["a_y"], 3)
                            sp.dma_start(rows(x_a, ca), axo).then_inc(S["a_st"], 16)
                        if s == "B_x2":
                            sp.wait_ge(S["b_x2"], 1)
                            sp.dma_start(rows(x_b, cb), bx2[:, :, :]).then_inc(S["b_st"], 16)
                        if s == "B_split":
                            sp.wait_ge(S["b_va"], 1)
                            sp.dma_start(v_tiles[bass.ds(cb * P, P), :],
                                         bva[:, :, :, :].rearrange("p t g v -> p (t g v)")).then_inc(S["b_st2"], 16)
                            sp.wait_ge(S["b_p"], 3)
                            for k, dram in enumerate((q_parts, k_parts)):
                                sp.dma_start(dram[bass.ds(cb * PARTS * P, PARTS * P), :]
                                             .rearrange("(s p) n -> p s n", s=PARTS),
                                             bp[:, :, k, :]).then_inc(S["b_st2"], 16)
                        if s == "C_max":
                            sp.wait_ge(S["c_mT"], 1)
                            for i in range(PARTS):
                                sp.dma_start(cQ[SROWS + i:SROWS + i + 1, :, :],
                                             cmT[i * H:(i + 1) * H, :]).then_inc(S["c_rows"], 16)
                        if s == "G_fin":
                            sp.wait_ge(S["c_y"], 1)
                            sp.dma_start(rows(x_c, cg), cxo).then_inc(S["c_st"], 16)
                        if s == "R_hn":
                            sp.wait_ge(S["r_hn"], 1)
                            sp.dma_start(rows(x_h, cr), rhn[:, :, :]).then_inc(S["r_st"], 16)
                        if s == "R_info":
                            sp.wait_ge(S["r_info"], 1)
                            sp.dma_start(info_d[bass.ds(cr * P, P), :],
                                         rinfo[:, :, :].rearrange("p t i -> p (t i)")).then_inc(S["r_st"], 16)
                        if s == "S_slot":
                            sp.wait_ge(S["s_slot"], 1)
                            sp.dma_start(slot_d[gs * GROUP * P:(gs + 1) * GROUP * P, :]
                                         .rearrange("(c p) i -> p c i", p=P),
                                         sslot[:, :, :, :].rearrange("p c k t -> p c (k t)")).then_inc(S["s_st"], 16)
                            sp.wait_ge(S["s_tile"], 1)
                            sp.dma_start(tile_d[gs], sei[0:1, :]).then_inc(S["s_st"], 16)
                        if s[:4] == "S_sc" and int(s[4:]) % 2 == 1 and int(s[4:]) // 2 + 2 < GROUP:
                            c = int(s[4:]) // 2
                            sp.wait_ge(S[f"s_sc{c % 2}"], 16 * 2 * NT * (gs * GROUP // 2 + c // 2 + 1))
                            load_sorted(sp, c + 2)
                        if s[:3] == "M_d" and int(s[3:]) + MW < MT:
                            t = int(s[3:])
                            sp.wait_ge(S["m_y"], t + 1)
                            load_weights(sp, t + MW)
                        if s == f"M_d{MT - 1}":
                            sp.wait_ge(S["m_o"], MT)
                            sp.dma_start(y_slots[gm][bass.ds(first * P, MT * P), :]
                                         .rearrange("(t p) d -> p t d", p=P), mY[:, :, :]).then_inc(S["m_st"], 16)
                        if s == "K_out":
                            sp.wait_ge(S["k_out"], 1)
                            sp.dma_start(rows(a["out"], ck), kg[:, 0, :, :]).then_inc(S["k_st"], 16)
                    if on["A"]:
                        sp.wait_ge(S["a_st"], 16)
                    if on["B"]:
                        sp.wait_ge(S["b_st"], 16)
                        sp.wait_ge(S["b_st2"], 48)
                    if on["C"]:
                        sp.wait_ge(S["c_rows"], 16 * PARTS)
                    if on["G"]:
                        sp.wait_ge(S["c_st"], 16)
                    if on["R"]:
                        sp.wait_ge(S["r_st"], 32)
                    if on["S"]:
                        sp.wait_ge(S["s_st"], 32)
                        for k in range(2):
                            sp.wait_ge(S[f"s_sc{k}"], 16 * 2 * NT * (gs + 1) * (GROUP // 2))
                    if on["M"]:
                        sp.wait_ge(S["m_st"], 16)
                    if on["K"]:
                        sp.wait_ge(S["k_st"], 16)
                    if live.get("Z"):
                        sp.wait_ge(S["s_zero"], 16 * len(live["Z"]))

                @block.gpsimd
                def _(pool):
                    def rstd(k, var, nth, out):
                        pool.wait_ge(S[k + "_var"], nth)
                        pool.tensor_tensor(out[:, :], var[:, :], half[:, :], ALU.pow).then_inc(S[k + "_rstd"], 1)

                    def diff(nth):
                        pool.wait_ge(S["a_xn"], nth)
                        if nth == 2:
                            pool.wait_ge(S["a_xr"], 1)
                        pool.tensor_tensor(adx[:, :, :], axn[:, :, 1:T + 1], axn[:, :, 0:T],
                                           ALU.subtract).then_inc(S["a_dx"], 1)

                    for s in order["Pool"]:
                        if s == "A_ln0s":
                            rstd("a", avar, 1, ars)
                        if s == "A_ln0n":
                            pool.wait_ge(S["a_h0"], 1)
                            pool.wait_ge(S["a_ldm"], 16)
                            pool.tensor_tensor(by_batch(ah[:, :, :]), by_batch(ah0[:, :, :]),
                                               per_batch(am[:, :, SA, :], ah), ALU.add).then_inc(S["a_h"], 1)
                        if s == "A_ln1s":
                            rstd("a", avar, 2, ars)
                        if s == "A_xn":
                            diff(1)
                        if s == "A_ln2s":
                            rstd("a", avar, 3, ars)
                        if s == "A_xn2":
                            diff(2)
                        if s == "A_out":
                            pool.wait_ge(S["a_y"], 1)
                            pool.tensor_tensor(by_batch(ay1), by_batch(ay0),
                                               per_batch(am[:, :, GA, :], ay0), ALU.mult).then_inc(S["a_y"], 1)
                            pool.wait_ge(S["a_y"], 2)
                            pool.tensor_tensor(axo, ay1, ax[:, :, :], ALU.add).then_inc(S["a_y"], 1)
                        if s == "B_ln0s":
                            rstd("b", bvar, 1, brs)
                        if s == "B_ln1s":
                            rstd("b", bvar, 2, brs)
                        if s == "B_split":
                            pool.wait_ge(S["b_p"], 1)
                            pool.wait_ge(S["b_qk"], 2)
                            pool.tensor_tensor(br1, bqk[:, :, :], bp[:, 0, :, :],
                                               ALU.subtract).then_inc(S["b_r"], 1)
                            pool.wait_ge(S["b_p"], 2)
                            pool.wait_ge(S["b_r"], 1)
                            pool.tensor_tensor(br2, br1, bp[:, 1, :, :],
                                               ALU.subtract).then_inc(S["b_r"], 1)
                        if s == "R_ln":
                            rstd("r", rvar, 1, rrs)
                        if s == "R_hn":
                            pool.wait_ge(S["r_h0"], 1)
                            pool.wait_ge(S["r_ldm"], 16)
                            pool.tensor_tensor(by_batch(rhn[:, :, :]), by_batch(rh0[:, :, :]),
                                               per_batch(rm[:, :, 0, :], rhn), ALU.add).then_inc(S["r_hn"], 1)
                        if s[:4] == "S_sc":
                            c, k = divmod(int(s[4:]), 2)
                            if k == 0:
                                if c == 0:
                                    pool.wait_ge(S["s_slot"], 1)
                                pool.wait_ge(S[f"s_ldx{c % 2}"], 16 * (c // 2 + 1))
                            for t in range(NT):
                                pool.indirect_dma_start(
                                    out=x_slots[gs],
                                    out_offset=bass.IndirectOffsetOnAxis(ap=sslot[:, c, k, t:t + 1], axis=0),
                                    in_=sx[:, c % 2, t, :], in_offset=None).then_inc(S[f"s_sc{c % 2}"], 16)
                        if s[:3] == "K_g":
                            k = int(s[3:])
                            if k == 0:
                                pool.wait_ge(S["k_lds"], 16)
                            for t in range(NT):
                                pool.indirect_dma_start(
                                    out=kg[:, k, t, :], out_offset=None, in_=y_slots[gk],
                                    in_offset=bass.IndirectOffsetOnAxis(ap=kslot[:, k, t:t + 1], axis=0)
                                ).then_inc(S["k_g"], 16)

                @block.scalar
                def _(act):
                    def feature_affine(k, nth, ps, out, c, cs, sh):
                        act.wait_ge(S[k + "_tp"], nth)
                        if nth == 1:
                            act.wait_ge(S[k + "_ldm"], 32)
                        for b in range(BC):
                            act.activation(out[:, b * T:(b + 1) * T], ps[:, b * T:(b + 1) * T], ACT.Identity,
                                           bias=c[:, b, sh:sh + 1], scale=c[:, b, cs:cs + 1]).then_inc(S[k + "_h"], 1)

                    for s in order["Activation"]:
                        if s in ("A_xn", "A_xn2"):
                            nth = 1 if s == "A_xn" else 2
                            w_, b_ = (LN1W, LN1B) if nth == 1 else (LN2W, LN2B)
                            act.wait_ge(S["a_tp"], nth)
                            src_ = AB[nth - 1]
                            act.activation(axn[:, :, 1:T + 1], src_[:, :].rearrange("p (b t) -> p b t", b=BC),
                                           ACT.Identity, bias=col[:, b_:b_ + 1],
                                           scale=col[:, w_:w_ + 1]).then_inc(S["a_xn"], 1)
                        if s == "A_r":
                            act.wait_ge(S["a_r"], 1)
                            act.activation(ath[:, :], AB[1][:, :], ACT.Tanh, scale=0.5).then_inc(S["a_th"], 1)
                        if s == "A_exp":
                            act.wait_ge(S["a_m"], 1)
                            act.activation(aP, amx, ACT.Exp, scale=-1.0).then_inc(S["a_exp"], 1)
                            act.wait_ge(S["a_m"], 2)
                            act.activation(aQ[:, 1:3, :, :], amn, ACT.Exp).then_inc(S["a_exp"], 1)
                        if s[:4] == "A_fk":
                            c = int(s[4:])
                            act.wait_ge(S["a_fk"], c + 1)
                            act.activation(arl[:, c, :], AB[c % 2][:, :], ACT.Relu).then_inc(S["a_rl"], 1)
                            act.wait_ge(S["a_rl"], c + 1)
                            act.activation(asq[:, c, :], arl[:, c, :], ACT.Square).then_inc(S["a_sq"], 1)
                        if s == "A_fr":
                            act.wait_ge(S["a_fr"], 1)
                            act.activation(ath2, AB[0][:, :], ACT.Tanh, scale=0.5).then_inc(S["a_th2"], 1)
                        if s == "B_h":
                            feature_affine("b", 1, BB, bh, bc, CB0, SB0)
                        if s[:4] == "B_w1":
                            c = int(s[4:])
                            act.wait_ge(S["b_w1"], c + 1)
                            act.activation(bhs[:, c, :], BB[:, :], ACT.Relu,
                                           bias=col[:, L0B1 + c:L0B1 + c + 1]).then_inc(S["b_hs"], 1)
                        if s == "B_h2":
                            feature_affine("b", 2, BB, bh, bc, CA1, SA1)
                        if s == "B_split":
                            act.wait_ge(S["b_qk"], 2)
                            act.activation(bp[:, 0, :, :], bqk[:, :, :], ACT.Copy).then_inc(S["b_p"], 1)
                            act.wait_ge(S["b_r"], 1)
                            act.activation(bp[:, 1, :, :], br1, ACT.Copy).then_inc(S["b_p"], 1)
                            act.wait_ge(S["b_r"], 2)
                            act.activation(bp[:, 2, :, :], br2, ACT.Copy).then_inc(S["b_p"], 1)
                        if s == "C_max":
                            act.wait_ge(S["c_mt"], 1)
                            act.activation(cmT[:, :], CO[0:PARTS * H, 0:N // 2].bitcast(BF16),
                                           ACT.Copy).then_inc(S["c_mT"], 1)
                        if s.startswith("G_g"):
                            g0 = int(s[3:])
                            for m in range(4 * g0, 4 * g0 + 4):
                                act.wait_ge(S["c_s2"], m + 1)
                                if m >= 8:
                                    act.wait_ge(S["c_pv"], (m - 8) // 4 + 1)
                                act.activation(cP[:, m % 8, :], CS[m % 2][:, :], ACT.Exp,
                                               scale=SCALE).then_inc(S["c_p"], 1)
                        if s.startswith("G_o"):
                            o = int(s[3:])
                            act.wait_ge(S["c_pv"], 2 * o + 2)
                            if o:
                                act.wait_ge(S["c_ot"], o)
                            act.activation(cos_[:, :], CO[:, :], ACT.Copy).then_inc(S["c_o"], 1)
                        if s == "G_fin":
                            act.wait_ge(S["c_ct"], 1)
                            act.activation(ccT[:, :], CO[:, :], ACT.Copy).then_inc(S["c_cT"], 1)
                        if s == "R_h":
                            act.wait_ge(S["r_tp"], 1)
                            act.activation(rh[:, :], DB[:, :], ACT.Copy).then_inc(S["r_h"], 1)
                        if s == "R_e":
                            act.wait_ge(S["r_dm"], 1)
                            act.activation(re[:, :], rdm[:, :], ACT.Exp).then_inc(S["r_e"], 1)
                        if s[:3] == "M_t":
                            k = int(s[3:])
                            act.wait_ge(S["m_tp"], k + 1)
                            w_ = min(FC, MT - FC * k) * P
                            act.activation(mT[:, k * FC * P:k * FC * P + w_], MB[:, 0:w_],
                                           ACT.Copy).then_inc(S["m_x"], 1)
                        if s[:3] == "M_u":
                            t = int(s[3:])
                            act.wait_ge(S["m_h"], t + 1)
                            for c in range(FC):
                                act.activation(mH[:, c * P:(c + 1) * P], MB[:, c * P:(c + 1) * P], ACT.Relu,
                                               bias=mW[:, t % MW, FC * P + c:FC * P + c + 1]).then_inc(S["m_r"], 1)
                        if s[:3] == "M_d":
                            t = int(s[3:])
                            act.wait_ge(S["m_y"], t + 1)
                            act.activation(mY[:, t, :], MB[:, 0:P], ACT.Copy).then_inc(S["m_o"], 1)
                        if s == "K_w":
                            act.wait_ge(S["k_tp"], 1)
                            act.activation(kwT[:, :], DB[0:EXPERTS, :], ACT.Copy).then_inc(S["k_wT"], 1)

                @block.tensor
                def _(pe):
                    def turn(k, nth, src_, ps):
                        pe.wait_ge(S[k + "_norm"], NT * nth)
                        for t in range(NT):
                            ins = pe.transpose(ps[:, t * P:(t + 1) * P], src_[:, t, :], ident[:, :])
                        ins.then_inc(S[k + "_tp"], 1)

                    def bias_rows(ps, r):
                        pe.matmul(ps[:, :], ones3[:, :],
                                  brow[:, r * D:(r + 1) * D].unsqueeze(1).broadcast_to([PARTS, NT, D]),
                                  start=True, stop=False)

                    def weigh(g0):
                        if g0 % 2 == 0 and g0:
                            pe.wait_ge(S["c_ctx"], g0 // 2)
                        if g0 == 0:
                            pe.wait_ge(S["c_ldv"], 16)
                        pe.wait_ge(S["c_p"], 4 * g0 + 4)
                        b, sc_ = g0 // 4, g0 % 2
                        for g in range(KV):
                            ins = pe.matmul(CO[32 * g:32 * g + 32, :], cV[:, b * 2 + sc_, g, :],
                                            cP[:, (4 * g0 + g) % 8, :], start=(sc_ == 0), stop=(sc_ == 1))
                        ins.then_inc(S["c_pv"], 1)

                    for s in order["PE"]:
                        if s == "A_xn":
                            turn("a", 1, az, AB[0])
                        if s == "A_r":
                            pe.wait_ge(S["a_xr"], 1)
                            pe.matmul(AB[1][:, :], wr[:, :], axr[:, :, :].rearrange("p b t -> p (b t)"),
                                      start=True, stop=True).then_inc(S["a_r"], 1)
                        if s == "A_k":
                            pe.wait_ge(S["a_xk"], 1)
                            pe.matmul(AB[0][:, :], wk[:, :], axk[:, :, :].rearrange("p b t -> p (b t)"),
                                      start=True, stop=True).then_inc(S["a_k"], 1)
                        if s == "A_v":
                            pe.wait_ge(S["a_xv"], 1)
                            pe.wait_ge(S["a_th"], 1)
                            pe.matmul(AB[1][:, :], wv[:, :], axv[:, :, :].rearrange("p b t -> p (b t)"),
                                      start=True, stop=True).then_inc(S["a_v"], 1)
                        if s == "A_wo":
                            pe.wait_ge(S["a_att"], 1)
                            for t in range(NT):
                                ins = pe.matmul(AB[0][:, t * P:(t + 1) * P], aatt[:, t * P:(t + 1) * P], wo[:, :],
                                                start=True, stop=True)
                            ins.then_inc(S["a_wo"], 1)
                        if s == "A_xn2":
                            turn("a", 2, az, AB[1])
                        if s[:4] == "A_fk":
                            c = int(s[4:])
                            if c == 0:
                                pe.wait_ge(S["a_xk"], 2)
                            elif c == 1:
                                pe.wait_ge(S["a_xn"], 2)
                            else:
                                pe.wait_ge(S["a_rl"], c - 1)
                            pe.matmul(AB[c % 2][:, :], fwk[:, c * P:(c + 1) * P],
                                      axk[:, :, :].rearrange("p b t -> p (b t)"),
                                      start=True, stop=True).then_inc(S["a_fk"], 1)
                        if s == "A_fr":
                            pe.wait_ge(S["a_xr"], 2)
                            pe.wait_ge(S["a_rl"], 3)
                            x_ = axr[:, :, :].rearrange("p b t -> p (b t)")
                            for t in range(NT):
                                ins = pe.matmul(AB[0][:, t * P:(t + 1) * P], x_[:, t * P:(t + 1) * P], fwr[:, :],
                                                start=True, stop=True)
                            ins.then_inc(S["a_fr"], 1)
                        if s[:4] == "A_vk":
                            k = int(s[4:])
                            pe.wait_ge(S["a_sq"], FC)
                            for t in range(2 * k, 2 * k + 2):
                                for c in range(FC):
                                    ins = pe.matmul(AB[1][:, t * P:(t + 1) * P], asq[:, c, t * P:(t + 1) * P],
                                                    fwv[:, c, :], start=(c == 0), stop=(c == FC - 1))
                            ins.then_inc(S["a_vk"], 1)
                        if s == "B_h":
                            turn("b", 1, bz, BB)
                        if s[:4] == "B_w1":
                            c = int(s[4:])
                            if c == 0:
                                pe.wait_ge(S["b_h"], 2)
                            else:
                                pe.wait_ge(S["b_hs"], c)
                            pe.matmul(BB[:, :], w1[:, c * P:(c + 1) * P], bh[:, :],
                                      start=True, stop=True).then_inc(S["b_w1"], 1)
                        if s[:4] == "B_w2":
                            k = int(s[4:])
                            if k == 0:
                                pe.wait_ge(S["b_hs"], FC)
                                bias_rows(BB, B2)
                            for t in range(2 * k, 2 * k + 2):
                                for c in range(FC):
                                    ins = pe.matmul(BB[:, t * P:(t + 1) * P], bhs[:, c, t * P:(t + 1) * P],
                                                    w2[:, c, :], start=False, stop=(c == FC - 1 and t == NT - 1))
                            ins.then_inc(S["b_w2"], 1)
                        if s == "B_h2":
                            turn("b", 2, bz, BB)
                        if s[:3] == "B_q":
                            j = int(s[3:])
                            if j == 0:
                                pe.wait_ge(S["b_h"], 4)
                            else:
                                pe.wait_ge(S["b_t"], j)
                            pe.matmul(BB[:, :], (wqT, wqrT, wkT, wkrT)[j][:, :], bh[:, :],
                                      start=True, stop=True).then_inc(S["b_q"], 1)
                        if s == "B_v":
                            pe.wait_ge(S["b_t"], 4)
                            for t in range(NT):
                                ins = pe.matmul(BB[:, t * 32:(t + 1) * 32], bh[:, t * P:(t + 1) * P], wvT[:, :],
                                                start=True, stop=True)
                            ins.then_inc(S["b_v"], 1)
                        if s.startswith("C_s"):
                            u = int(s[3:])
                            if u == 0:
                                pe.wait_ge(S["c_ldq"], 16 * 2 * PARTS)
                                if on["G"]:
                                    pe.wait_ge(S["c_p"], 32)
                            if u >= 2:
                                pe.wait_ge(S["c_mx"], u - 1)
                            bt, hp = divmod(u, H // 2)
                            b = bt // 2
                            for j in range(2):
                                h = 2 * hp + j
                                ins = pe.matmul(CS[u % 2][:, j * T:(j + 1) * T],
                                                cQ[0:SROWS, h, bt * P:(bt + 1) * P],
                                                cK[0:SROWS, h // G, b * T:(b + 1) * T], start=True, stop=True)
                            ins.then_inc(S["c_s"], 1)
                        if s == "C_max":
                            pe.wait_ge(S["c_mp"], 3)
                            if on["G"]:
                                pe.wait_ge(S["c_y"], 1)
                            for t in range(NT):
                                ins = pe.transpose(CO[0:PARTS * H, t * 64:(t + 1) * 64].bitcast(BF16),
                                                   cmp[:, t, :, :].rearrange("p s h -> p (s h)"), identb[:, :])
                            ins.then_inc(S["c_mt"], 1)
                        if s.startswith("G_g"):
                            g0 = int(s[3:])
                            bp_, sc_ = divmod(g0, 2)
                            b, pp = divmod(bp_, 2)
                            for g in range(KV):
                                m = 4 * g0 + g
                                if m >= 2:
                                    pe.wait_ge(S["c_p"], m - 1)
                                h0 = g * G + pp * 2
                                pe.matmul(CS[m % 2][:, :],
                                          cK[0:KROWS, g, b * T + sc_ * P:b * T + (sc_ + 1) * P],
                                          cQ[0:KROWS, h0:h0 + 2, b * T:(b + 1) * T],
                                          start=True, stop=True).then_inc(S["c_s2"], 1)
                            if g0:
                                weigh(g0 - 1)
                            if g0 == 7:
                                weigh(7)
                        if s.startswith("G_o"):
                            o = int(s[3:])
                            pe.wait_ge(S["c_o"], o + 1)
                            for j in range(4):
                                ins = pe.transpose(CO[:, j * P:(j + 1) * P], cos_[:, j * P:(j + 1) * P], ident[:, :])
                            ins.then_inc(S["c_ot"], 1)
                        if s == "G_fin":
                            pe.wait_ge(S["c_ctx"], 4)
                            for t in range(NT):
                                ins = pe.transpose(CO[:, t * P:(t + 1) * P],
                                                   cctx[:, t, :, :, :, :].rearrange("p g a b d -> p (g a b d)"),
                                                   ident[:, :])
                            ins.then_inc(S["c_ct"], 1)
                            pe.wait_ge(S["c_cT"], 1)
                            bias_rows(CO, BO)
                            for t in range(NT):
                                ins = pe.matmul(CO[:, t * P:(t + 1) * P], ccT[:, t * P:(t + 1) * P], woT[:, :],
                                                start=False, stop=(t == NT - 1))
                            ins.then_inc(S["c_wo"], 1)
                        if s == "R_h":
                            pe.wait_ge(S["r_hn"], 1)
                            for t in range(NT):
                                ins = pe.transpose(DB[:, t * P:(t + 1) * P], rhn[:, t, :], ident[:, :])
                            ins.then_inc(S["r_tp"], 1)
                        if s == "R_lg":
                            pe.wait_ge(S["r_h"], 1)
                            for t in range(NT):
                                ins = pe.matmul(DB[:, t * EXPERTS:(t + 1) * EXPERTS], rh[:, t * P:(t + 1) * P],
                                                wrt[:, :], start=True, stop=True)
                            ins.then_inc(S["r_rt"], 1)
                        if s == "S_pre":
                            if on["R"]:
                                pe.wait_ge(S["r_lg"], 1)
                            pe.wait_ge(S["s_tot"], 1)
                            pe.matmul(DB[:, 0:EXPERTS], upper[:, :], stot[:, :], start=True, stop=True)
                            pe.matmul(DB[:, EXPERTS:2 * EXPERTS], onesf[:, :], stot[:, :], start=True,
                                      stop=True).then_inc(S["s_pre"], 1)
                        if s[:3] == "M_t":
                            k = int(s[3:])
                            if k == 0:
                                pe.wait_ge(S["m_ldx"], 16)
                            else:
                                pe.wait_ge(S["m_x"], k)
                            for j in range(min(FC, MT - FC * k)):
                                ins = pe.transpose(MB[:, j * P:(j + 1) * P], mX[:, FC * k + j, :], ident[:, :])
                            ins.then_inc(S["m_tp"], 1)
                        if s[:3] == "M_u":
                            t = int(s[3:])
                            if t == 0:
                                pe.wait_ge(S["m_x"], -(-MT // FC))
                            else:
                                pe.wait_ge(S["m_o"], t)
                            pe.wait_ge(S[f"m_w{t % MW}"], 16 * (t // MW + 1))
                            for c in range(FC):
                                ins = pe.matmul(MB[:, c * P:(c + 1) * P], mW[:, t % MW, c * P:(c + 1) * P],
                                                mT[:, t * P:(t + 1) * P], start=True, stop=True)
                            ins.then_inc(S["m_h"], 1)
                        if s[:3] == "M_d":
                            t = int(s[3:])
                            pe.wait_ge(S["m_r"], FC * (t + 1))
                            for c in range(FC):
                                w_ = FC * P + FC + c * D
                                ins = pe.matmul(MB[:, 0:P], mH[:, c * P:(c + 1) * P], mW[:, t % MW, w_:w_ + D],
                                                start=(c == 0), stop=(c == FC - 1))
                            ins.then_inc(S["m_y"], 1)
                        if s == "K_w":
                            if on["R"]:
                                pe.wait_ge(S["r_lg"], 1)
                            if on["S"]:
                                pe.wait_ge(S["s_slot"], 1)
                            pe.wait_ge(S["k_ldi"], 16)
                            for t in range(NT):
                                ins = pe.transpose(DB[0:EXPERTS, t * P:(t + 1) * P], kinfo[:, t, WT:WT + EXPERTS],
                                                   ident[:, :])
                            ins.then_inc(S["k_tp"], 1)
                        if s == "K_b":
                            pe.wait_ge(S["k_wT"], 1)
                            for t in range(NT):
                                ins = pe.matmul(DB[:, t * P:(t + 1) * P], kwT[:, t * P:(t + 1) * P], eb2[:, :],
                                                start=True, stop=True)
                            ins.then_inc(S["k_b"], 1)

                @block.vector
                def _(dve):
                    av = Count(dve, S["a_vec"])
                    bv_ = Count(dve, S["b_vec"])
                    cv = Count(dve, S["c_vec"])
                    rv = Count(dve, S["r_vec"])
                    sv = Count(dve, S["s_vec"])
                    kv_ = Count(dve, S["k_vec"])

                    def stats(k, c, src_, st, mv, var):
                        for t in range(NT):
                            c(dve.bn_stats(st[:, t, :], src_[:, t, :]))
                        c.wait()
                        for t in range(NT):
                            c(dve.bn_aggr(mv[:, t, :], st[:, t, :]))
                        c.wait()
                        dve.tensor_scalar(var[:, :], mv[:, :, 1], EPS, None, ALU.add).then_inc(S[k + "_var"], 1)

                    def norm(k, src_, mv, out_z, rs, nth):
                        dve.wait_ge(S[k + "_rstd"], nth)
                        for t in range(NT):
                            dve.tensor_scalar(out_z[:, t, :], src_[:, t, :], mv[:, t, 0:1], rs[:, t:t + 1],
                                              ALU.subtract, ALU.mult).then_inc(S[k + "_norm"], 1)

                    def mix(nth, which):
                        dve.wait_ge(S["a_dx"], nth)
                        for out_, m_, ev in which:
                            dve.scalar_tensor_tensor(out_[:, :, :], adx[:, :, :], col[:, m_:m_ + 1],
                                                     axn[:, :, 0:T], ALU.mult, ALU.add).then_inc(S[ev], 1)

                    k_ps = AB[0][:, :].rearrange("p (b t) -> p b t", b=BC)
                    b_ps = BB[:, :].rearrange("p (b t) -> p b t", b=BC)
                    v_ps = AB[1][:, :].rearrange("p (b t) -> p b t", b=BC)

                    def apart(x_):
                        return x_.rearrange("p (b t) -> p b t", b=BC)

                    def every(x_):
                        return x_[:, :].unsqueeze(1).broadcast_to([P, BC, T])

                    def over(x_):
                        return x_.unsqueeze(2).broadcast_to([P, NT, EXPERTS])

                    revb = rev[:, :].unsqueeze(1).broadcast_to([P, NT, EXPERTS])

                    def first_max(lg, m_, oh):
                        rv(dve.tensor_reduce(m_[:, :], lg[:, :, :], AX_X, ALU.max))
                        rv.wait()
                        rv(dve.tensor_tensor(req[:, :, :], lg[:, :, :], over(m_[:, :]), ALU.is_equal))
                        rv.wait()
                        rv(dve.tensor_tensor(req[:, :, :], req[:, :, :], revb, ALU.mult))
                        rv.wait()
                        rv(dve.tensor_reduce(ri[:, :], req[:, :, :], AX_X, ALU.max))
                        rv.wait()
                        rv(dve.tensor_tensor(oh, revb, over(ri[:, :]), ALU.is_equal))
                        rv.wait()

                    def s_oh(k):
                        return sinfo[:, :, :].rearrange("p c (t i) -> p c t i", t=NT)[:, :, :, k:k + EXPERTS]

                    def by_expert(x_):
                        return x_[:, :, :].rearrange("p e (c t) -> p c t e", c=GROUP)

                    for s in order["DVE"]:
                        if s == "A_ln0s":
                            dve.wait_ge(S["a_ld"], 16)
                            stats("a", av, ax, ast, amv, avar)
                        if s == "A_ln0n":
                            dve.wait_ge(S["a_rstd"], 1)
                            for t in range(NT):
                                av(dve.tensor_scalar(az[:, t, :], ax[:, t, :], amv[:, t, 0:1], ars[:, t:t + 1],
                                                     ALU.subtract, ALU.mult))
                            av.wait()
                            dve.wait_ge(S["a_ldm"], 16)
                            dve.tensor_tensor(by_batch(ah0[:, :, :]), by_batch(az[:, :, :]),
                                              per_batch(am[:, :, CA, :], az), ALU.mult).then_inc(S["a_h0"], 1)
                        if s == "A_ln1s":
                            dve.wait_ge(S["a_h"], 1)
                            dve.wait_ge(S["a_h0"], 1)
                            stats("a", av, ah, ast, amv, avar)
                        if s == "A_ln1n":
                            norm("a", ah, amv, az, ars, 2)
                        if s == "A_mix":
                            mix(1, ((axr, MIXR, "a_xr"), (axk, MIXK, "a_xk"), (axv, MIXV, "a_xv")))
                        if s == "A_scan":
                            dve.wait_ge(S["a_k"], 1)
                            for b in range(BC):
                                av(dve.tensor_tensor_scan(aE[:, b, 1:T + 1], negw[:, 0:1].broadcast_to([P, T]),
                                                          k_ps[:, b, :], NEG_INIT, ALU.add, ALU.max))
                            av.wait()
                        if s == "A_y":
                            av(dve.scalar_tensor_tensor(azy[:, 0, :, :], k_ps, col[:, FIRST:FIRST + 1],
                                                        aE[:, :, 0:T], ALU.add, ALU.subtract))
                            av(dve.scalar_tensor_tensor(azy[:, 1, :, :], aE[:, :, 0:T], negw[:, 0:1],
                                                        k_ps, ALU.add, ALU.subtract))
                            av.wait()
                            dve.tensor_scalar(amx, azy, 0.0, None,
                                              ALU.max).then_inc(S["a_m"], 1)
                            dve.tensor_scalar(amn, azy, 0.0, None,
                                              ALU.min).then_inc(S["a_m"], 1)
                        if s == "A_wkv":
                            dve.wait_ge(S["a_v"], 1)
                            dve.wait_ge(S["a_exp"], 1)
                            av(dve.tensor_tensor(ad2v, aP[:, 1, :, :], v_ps, ALU.mult))
                            dve.wait_ge(S["a_exp"], 2)
                            av(dve.tensor_tensor(aQ[:, 0, :, :], aQ[:, 1, :, :], v_ps, ALU.mult))
                            av.wait()
                        if s == "A_wkv1":
                            for j, add in enumerate((ad2v, aP[:, 1, :, :])):
                                for b in range(BC):
                                    av(dve.tensor_tensor_scan(aAB[:, j, b, 1:T + 1], aQ[:, 2, b, :], add[:, b, :],
                                                              0.0, ALU.mult, ALU.add))
                            av.wait()
                        if s == "A_wkv2":
                            for j in range(2):
                                av(dve.tensor_tensor(and1[:, j, :, :], aAB[:, j, :, 0:T], aP[:, 0, :, :], ALU.mult))
                            av.wait()
                            av(dve.tensor_tensor(and2[:, :, :, :], and1[:, :, :, :], aQ[:, 0:2, :, :], ALU.add))
                            av.wait()
                        if s == "A_rec":
                            av(dve.reciprocal(ards, and2[:, 1, :, :].rearrange("p b t -> p (b t)")))
                            av.wait()
                        if s == "A_att":
                            av(dve.tensor_tensor(aw, and2[:, 0, :, :].rearrange("p b t -> p (b t)"), ards,
                                                 ALU.mult))
                            av.wait()
                            dve.wait_ge(S["a_th"], 1)
                            dve.scalar_tensor_tensor(aatt, ath[:, :], 1.0, aw, ALU.add,
                                                     ALU.mult).then_inc(S["a_att"], 1)
                        if s == "A_wo":
                            dve.wait_ge(S["a_wo"], 1)
                            dve.tensor_tensor(ax1[:, :, :], ah[:, :, :], tiles(AB[0]), ALU.add).then_inc(S["a_x1"], 1)
                        if s == "A_ln2s":
                            dve.wait_ge(S["a_x1"], 1)
                            stats("a", av, ax1, ast, amv, avar)
                        if s == "A_ln2n":
                            norm("a", ax1, amv, az, ars, 3)
                        if s == "A_mix2":
                            mix(2, ((axk, FMIXK, "a_xk"), (axr, FMIXR, "a_xr")))
                        if s == "A_out":
                            dve.wait_ge(S["a_th2"], 1)
                            dve.wait_ge(S["a_vk"], 2)
                            av(dve.scalar_tensor_tensor(aq, ath2, 1.0, AB[1][:, :], ALU.add, ALU.mult))
                            av.wait()
                            dve.tensor_tensor(ay0, ax1[:, :, :], aq.rearrange("p (t d) -> p t d", d=D), ALU.add).then_inc(S["a_y"], 1)
                        if s == "B_ln0s":
                            dve.wait_ge(S["b_ld"], 16)
                            stats("b", bv_, bx, bst, bmv, bvar)
                        if s == "B_ln0n":
                            norm("b", bx, bmv, bz, brs, 1)
                        if s == "B_x2":
                            dve.wait_ge(S["b_w2"], 2)
                            dve.wait_ge(S["b_ldm"], 32)
                            bv_(dve.tensor_tensor(by_batch(by[:, :, :]), by_batch(tiles(BB)),
                                                  per_batch(bm[:, :, :], by), ALU.mult))
                            bv_.wait()
                            dve.tensor_tensor(bx2[:, :, :], bx[:, :, :], by[:, :, :], ALU.add).then_inc(S["b_x2"], 1)
                        if s == "B_ln1s":
                            dve.wait_ge(S["b_x2"], 1)
                            stats("b", bv_, bx2, bst, bmv, bvar)
                        if s == "B_ln1n":
                            norm("b", bx2, bmv, bz, brs, 2)
                        if s[:3] == "B_q":
                            j = int(s[3:])
                            b_, tab, out_ = ((col[:, BQ:BQ + 1], cos, bt1), (bqr[:, 0:1], sin, bt2),
                                             (col[:, BK:BK + 1], cos, bt1), (bkr[:, 0:1], sin, bt2))[j]
                            if j == 2:
                                dve.wait_ge(S["b_qk"], 1)
                            dve.wait_ge(S["b_q"], j + 1)
                            dve.scalar_tensor_tensor(apart(out_), b_ps, b_, every(tab), ALU.add,
                                                     ALU.mult).then_inc(S["b_t"], 1)
                            if j % 2:
                                dve.wait_ge(S["b_t"], j + 1)
                                dve.tensor_tensor(bqk[:, j // 2, :], bt1, bt2, ALU.add).then_inc(S["b_qk"], 1)
                        if s == "B_v":
                            dve.wait_ge(S["b_v"], 1)
                            dve.tensor_tensor(bva[:, :, :, 0:HD],
                                              BB[:, 0:NT * 32].rearrange("p (t g v) -> p t g v", t=NT, g=KV),
                                              bv[:, :].rearrange("p (g v) -> p g v", g=KV).unsqueeze(1)
                                              .broadcast_to([P, NT, KV, HD]), ALU.add).then_inc(S["b_va"], 1)
                        if s.startswith("C_s"):
                            u = int(s[3:])
                            bt, hp = divmod(u, H // 2)
                            dve.wait_ge(S["c_s"], u + 1)
                            dve.tensor_reduce(cmx[:, bt, 2 * hp:2 * hp + 2],
                                              CS[u % 2][:, :].rearrange("p (j t) -> p j t", j=2), AX_X, ALU.max,
                                              negate=True).then_inc(S["c_mx"], 1)
                        if s == "C_max":
                            dve.wait_ge(S["c_mx"], 32)
                            dve.tensor_copy(cmp[:, :, 0, :], cmx[:, :, :]).then_inc(S["c_mp"], 1)
                            dve.wait_ge(S["c_mp"], 1)
                            cv(dve.tensor_tensor(cr1[:, :, :], cmx[:, :, :], cmp[:, :, 0, :], ALU.subtract))
                            cv.wait()
                            dve.tensor_copy(cmp[:, :, 1, :], cr1[:, :, :]).then_inc(S["c_mp"], 1)
                            dve.wait_ge(S["c_mp"], 2)
                            cv(dve.tensor_tensor(cr2[:, :, :], cr1[:, :, :], cmp[:, :, 1, :], ALU.subtract))
                            cv.wait()
                            dve.tensor_copy(cmp[:, :, 2, :], cr2[:, :, :]).then_inc(S["c_mp"], 1)
                        if s.startswith("G_o"):
                            o = int(s[3:])
                            b, pp = divmod(o, 2)
                            dve.wait_ge(S["c_ot"], o + 1)
                            t_ = CO[:, :].rearrange("p (j t g v) -> p j t g v", j=2, t=2, g=KV)
                            cv(dve.reciprocal(crs[:, :, :], CO[:, :].rearrange("p (j g v) -> p j g v", j=4, g=KV)[:, :, :, HD]))
                            cv.wait()
                            for j in range(2):
                                ins = dve.tensor_tensor(cctx[:, 2 * b:2 * b + 2, :, pp, j, :], t_[:, j, :, :, 0:HD],
                                                        crs[:, 2 * j:2 * j + 2, :].unsqueeze(3)
                                                        .broadcast_to([P, 2, KV, HD]), ALU.mult)
                                if j:
                                    ins.then_inc(S["c_ctx"], 1)
                        if s == "G_fin":
                            dve.wait_ge(S["c_wo"], 1)
                            dve.wait_ge(S["c_ldm"], 32)
                            cv(dve.tensor_tensor(by_batch(cy), by_batch(tiles(CO)),
                                                 per_batch(cm[:, :, :], cy), ALU.mult))
                            cv.wait()
                            dve.tensor_tensor(cxo, cx[:, :, :], cy, ALU.add).then_inc(S["c_y"], 1)
                        if s == "R_ln":
                            dve.wait_ge(S["r_ld"], 16)
                            stats("r", rv, rx, rst, rmv, rvar)
                        if s == "R_hn":
                            norm("r", rx, rmv, rz, rrs, 1)
                            dve.wait_ge(S["r_norm"], NT)
                            dve.wait_ge(S["r_ldm"], 16)
                            dve.tensor_tensor(by_batch(rh0[:, :, :]), by_batch(rz[:, :, :]),
                                              per_batch(rm[:, :, 1, :], rz), ALU.mult).then_inc(S["r_h0"], 1)
                        if s == "R_lg":
                            dve.wait_ge(S["r_rt"], 1)
                            dve.tensor_tensor(rlg[:, :, :],
                                              DB[:, 0:NT * EXPERTS].rearrange("p (t e) -> p t e", t=NT),
                                              brt[:, :].unsqueeze(1).broadcast_to([P, NT, EXPERTS]),
                                              ALU.add).then_inc(S["r_lg"], 1)
                        if s == "R_m1":
                            dve.wait_ge(S["r_lg"], 1)
                            first_max(rlg, rm1, rinfo[:, :, OH1:OH1 + EXPERTS])
                            rv(dve.scalar_tensor_tensor(rlg2[:, :, :], rinfo[:, :, OH1:OH1 + EXPERTS], -3e38,
                                                        rlg[:, :, :], ALU.mult, ALU.add))
                            rv.wait()
                        if s == "R_m2":
                            first_max(rlg2, rm2, rinfo[:, :, OH2:OH2 + EXPERTS])
                        if s == "R_e":
                            dve.tensor_tensor(rdm[:, :], rm2[:, :], rm1[:, :], ALU.subtract).then_inc(S["r_dm"], 1)
                        if s == "R_info":
                            dve.wait_ge(S["r_e"], 1)
                            rv(dve.tensor_scalar(rp[:, :], re[:, :], 1.0, None, ALU.add))
                            rv.wait()
                            rv(dve.reciprocal(rinfo[:, :, P1], rp[:, :]))
                            rv.wait()
                            rv(dve.tensor_tensor(rinfo[:, :, P2], rinfo[:, :, P1], re[:, :], ALU.mult))
                            rv(dve.tensor_tensor(rw1[:, :, :], rinfo[:, :, OH1:OH1 + EXPERTS],
                                                 over(rinfo[:, :, P1]), ALU.mult))
                            rv.wait()
                            rv(dve.tensor_tensor(rw2[:, :, :], rinfo[:, :, OH2:OH2 + EXPERTS],
                                                 over(rinfo[:, :, P2]), ALU.mult))
                            rv.wait()
                            dve.tensor_tensor(rinfo[:, :, WT:WT + EXPERTS], rw1[:, :, :], rw2[:, :, :],
                                              ALU.add).then_inc(S["r_info"], 1)
                        if s == "S_cnt":
                            dve.wait_ge(S["s_ld"], 16)
                            sv(dve.tensor_tensor(by_expert(scnt), s_oh(OH1), s_oh(OH2), ALU.add))
                            sv.wait()
                            sv(dve.tensor_tensor_scan(sinc[:, :, :].rearrange("p e j -> p (e j)"), restart[:, :],
                                                      scnt[:, :, :].rearrange("p e j -> p (e j)"), 0.0,
                                                      ALU.mult, ALU.add))
                            sv.wait()
                            dve.tensor_copy(stot[:, :], sinc[:, :, GT - 1]).then_inc(S["s_tot"], 1)
                            sv(dve.tensor_tensor(spos[:, :, :], sinc[:, :, :], scnt[:, :, :], ALU.subtract))
                        if s == "S_base":
                            dve.wait_ge(S["s_pre"], 1)
                            sv(dve.tensor_copy(snum[:, :], DB[:, EXPERTS:2 * EXPERTS]))
                            sv.wait()
                            sv(dve.tensor_tensor(scmp[:, :, :],
                                                 steps16[:, :].unsqueeze(1).broadcast_to([P, EXPERTS, GT]),
                                                 snum[:, :].unsqueeze(2).broadcast_to([P, EXPERTS, GT]), ALU.is_lt))
                            sv.wait()
                            sv(dve.tensor_reduce(snt[:, :], scmp[:, :, :], AX_X, ALU.add))
                            sv.wait()
                            sv(dve.tensor_tensor_scan(sti[:, :], sone[:, :], snt[:, :], 0.0, ALU.mult, ALU.add))
                            sv.wait()
                            sv(dve.tensor_tensor(sbase[:, :], sti[:, :], snt[:, :], ALU.subtract))
                            sv.wait()
                            sv(dve.scalar_tensor_tensor(sbase[:, :], sbase[:, :], float(P), DB[:, 0:EXPERTS],
                                                        ALU.mult, ALU.add))
                            sv.wait()
                            sv(dve.tensor_tensor(spos[:, :, :], spos[:, :, :],
                                                 sbase[:, :].unsqueeze(2).broadcast_to([P, EXPERTS, GT]), ALU.add))
                            sv.wait()
                        if s == "S_slot":
                            for k, oh in enumerate((OH1, OH2)):
                                sv(dve.tensor_tensor(sprod[:, :, :].rearrange("p (c t) e -> p c t e", c=GROUP),
                                                     s_oh(oh), by_expert(spos), ALU.mult))
                                sv.wait()
                                sv(dve.tensor_reduce(sslf[:, k, :], sprod[:, :, :], AX_X, ALU.add))
                                sv.wait()
                            dve.tensor_copy(sslot[:, :, :, :],
                                            sslf[:, :, :].rearrange("p k (c t) -> p c k t", c=GROUP)
                                            ).then_inc(S["s_slot"], 1)
                            sv(dve.tensor_tensor(scm2[:, :, :],
                                                 sti[:, :].unsqueeze(1).broadcast_to([P, SLOT_TILES, EXPERTS]),
                                                 steps1[:, :].unsqueeze(2).broadcast_to([P, SLOT_TILES, EXPERTS]),
                                                 ALU.is_le))
                            sv.wait()
                            sv(dve.tensor_reduce(sef[:, :], scm2[:, :, :], AX_X, ALU.add))
                            sv.wait()
                            sv(dve.tensor_scalar(sef[:, :], sef[:, :], float(EXPERTS - 1), float(P),
                                                 ALU.min, ALU.mult))
                            sv.wait()
                            dve.tensor_copy(sei[:, :], sef[:, :]).then_inc(S["s_tile"], 1)
                        if s == "K_sum":
                            dve.wait_ge(S["k_g"], (ck + 1) * (16 * 2 * NT))
                            dve.wait_ge(S["k_ldi"], 16)
                            for t in range(NT):
                                kv_(dve.tensor_scalar(kacc[:, t, :], kg[:, 0, t, :], kinfo[:, t, P1:P1 + 1], None,
                                                      ALU.mult))
                            kv_.wait()
                            for t in range(NT):
                                kv_(dve.scalar_tensor_tensor(kacc[:, t, :], kg[:, 1, t, :],
                                                             kinfo[:, t, P2:P2 + 1], kacc[:, t, :],
                                                             ALU.mult, ALU.add))
                            kv_.wait()
                        if s == "K_out":
                            dve.wait_ge(S["k_b"], 1)
                            dve.wait_ge(S["k_ldx"], 32)
                            kv_(dve.tensor_tensor(kacc, kacc, tiles(DB), ALU.add))
                            kv_.wait()
                            kv_(dve.tensor_tensor(by_batch(kg[:, 1, :, :]), by_batch(kacc),
                                                  per_batch(km[:, :, :], kacc), ALU.mult))
                            kv_.wait()
                            dve.tensor_tensor(kg[:, 0, :, :], kx[:, :, :], kg[:, 1, :, :],
                                              ALU.add).then_inc(S["k_out"], 1)

            new_round()

        def parts_of(n):
            r = {k: True for s, k in enumerate("ABCGR") if 0 <= n - s < CHUNKS}
            for k, first in (("M", FIRST_TILES), ("K", FIRST_SUM)):
                if first <= n < first + CHUNKS:
                    r[k] = (n - first) // GROUP
            if n >= FIRST_SORT and (n - FIRST_SORT) % GROUP == 0 and (n - FIRST_SORT) // GROUP < GROUPS:
                r["S"] = (n - FIRST_SORT) // GROUP
            if n < STAGES - 1:
                r["Z"] = range(n, n + 1) if n < STAGES - 2 else range(n, GROUPS)
            return r

        n = 0
        while n < ROUNDS:
            end = n + 1
            while end < ROUNDS and parts_of(end) == parts_of(n):
                end += 1
            if end - n > 1:
                with nc.Fori(n, end) as i:
                    one_round(i, parts_of(n))
            else:
                one_round(n, parts_of(n))
            n = end


ROWS_DONE = 4 + 4 + 2 + 2 * (4 + 2 * 4) + MODC


SCHEDULE = {k: v.split() for k, v in {
    "SP": """
        R_ld R_ldm G_ldv B_ld B_ldm S_ld A_ld A_ldm R_hn K_lds M_lde G_ldm M_ldx M_ldw K_ldi C_ldq M_d0 S_slot
        R_info M_d1 M_d2 S_sc1 M_d3 S_sc3 K_ldx M_d4 M_d5 M_d6 M_d7 B_x2 B_split G_fin K_out A_out M_d9 C_max
        """,
    "Pool": """
        R_ln R_hn B_ln0s A_ln0s A_ln0n A_ln1s K_g0 K_g1 A_xn S_sc0 S_sc1 S_sc2 S_sc3 A_ln2s B_ln1s S_sc4 A_xn2 S_sc5
        S_sc6 S_sc7 B_split A_out
        """,
    "Activation": """
        G_g0 G_g1 G_g2 G_o0 G_g3 G_g4 G_o1 R_h A_xn G_g5 B_h G_g6 G_o2 G_g7 R_e M_t0 M_t1 A_r M_t2 B_w10 M_u0 A_exp
        B_w11 M_d0 M_u1 B_w12 M_d1 B_w13 G_o3 M_u2 K_w M_d2 M_u3 M_d3 M_u4 M_d4 M_u5 B_h2 A_xn2 M_d5 M_u6 A_fk0
        A_fk1 A_fk2 A_fk3 M_d6 M_u7 M_d7 G_fin B_split A_fr M_u8 M_d8 M_u9 M_d9 C_max
        """,
    "PE": """
        G_g0 G_g1 G_g2 R_h G_o0 G_g3 G_g4 A_xn B_h R_lg G_o1 G_g5 G_g6 M_t0 G_o2 G_g7 M_t1 A_r A_k M_t2 B_w10 M_u0
        C_s0 C_s1 A_v B_w11 M_d0 S_pre C_s2 C_s3 K_w M_u1 B_w12 M_d1 B_w13 M_u2 B_w20 C_s4 C_s5 M_d2 A_wo C_s6 M_u3
        B_w21 M_d3 C_s7 C_s8 M_u4 K_b C_s9 C_s10 M_d4 G_o3 M_u5 A_xn2 B_h2 C_s11 C_s12 M_d5 B_q0 C_s13 M_u6 B_q1
        A_fk0 A_fk1 A_fk2 C_s14 C_s15 A_fk3 M_d6 B_q2 M_u7 C_s16 C_s17 B_q3 C_s18 M_d7 C_s19 C_s20 G_fin C_s21 C_s22
        A_fr B_v C_s23 C_s24 A_vk0 C_s25 C_s26 M_u8 C_s27 C_s28 A_vk1 C_s29 M_d8 C_s30 M_u9 C_s31 M_d9 C_max
        """,
    "DVE": """
        R_ln R_hn B_ln0s A_ln0s A_ln0n G_o0 A_ln1s A_ln1n B_ln0n G_o1 R_lg R_m1 R_m2 R_e G_o2 A_mix R_info K_sum
        A_scan A_y C_s0 C_s1 A_wkv S_cnt S_base S_slot A_wkv1 A_wkv2 A_rec C_s2 C_s3 A_att C_s4 C_s5 A_wo A_ln2s
        C_s6 B_x2 C_s7 C_s8 B_ln1s A_ln2n B_ln1n C_s9 C_s10 C_s11 C_s12 B_q0 C_s13 A_mix2 B_q1 K_out C_s14 G_o3
        C_s15 B_q2 C_s16 C_s17 C_s18 B_q3 C_s19 C_s20 C_s21 C_s22 G_fin C_s23 C_s24 C_s25 C_s26 B_v C_s27 C_s28
        A_out C_s29 C_s30 C_s31 C_max
        """,
}.items()}


def kernel(**inputs):
    import ml_dtypes
    import concourse.bacc as _bacc
    from concourse import mybir as _mybir
    from concourse.bass_utils import run_bass_kernel_spmd as _run

    i = {k: np.ascontiguousarray(v) for k, v in inputs.items()}
    bf16 = ml_dtypes.bfloat16
    inv = (1.0 / 10000.0 ** (np.arange(0, HD, 2, dtype=np.float32) / HD)).astype(np.float32)
    ang = (np.arange(T, dtype=np.float32)[:, None] * inv[None, :]).astype(np.float32)
    by_q = [h * HD + d for d in range(HD) for h in range(H)]
    by_k = [h // G * HD + d for d in range(HD) for h in range(H)]
    by_row = [d % (HD // 2) for d in range(HD) for h in range(H)]
    cos = np.ascontiguousarray(np.cos(ang).T[by_row])
    sin = np.ascontiguousarray(np.sin(ang).T[by_row])
    rot = np.zeros((P, P), np.float32)
    for h in range(H):
        for r in range(HD // 2):
            rot[h * HD + 2 * r + 1, h * HD + r] = -1.0
            rot[h * HD + 2 * r, h * HD + HD // 2 + r] = 1.0
    rotk = rot[0:KV * HD][:, by_k]
    arrays = {k: v for k, v in i.items() if k in _PLAIN}
    arrays["x"] = i["L0_attn_x"].reshape(B * T, D)
    arrays["L1_attn_bv"] = i["L1_attn_bv"]
    arrays.update({
        "c_ident": np.eye(P, dtype=np.float32), "c_identb": np.eye(P).astype(bf16), "c_cos": cos, "c_sin": sin,
        "c_rotq": np.ascontiguousarray(rot[by_q][:, by_q]), "c_rotk": np.ascontiguousarray(rotk),
        "c_rev": np.tile(np.arange(EXPERTS, 0, -1, dtype=np.float32), (P, 1)),
        "c_ones3": np.ones((PARTS, P), bf16), "c_mask3": np.eye(PARTS, dtype=np.float32),
        "c_onesk": np.ones((PARTS, KV * N), bf16),
        "c_upper": np.triu(np.ones((P, P), np.float32), 1),
        "c_restart": np.tile(np.arange(GT) > 0, (P, EXPERTS)).astype(np.float32),
        "c_steps16": np.tile(np.arange(GT, dtype=np.float32) * P, (P, 1)),
        "c_steps1": np.tile(np.arange(SLOT_TILES, dtype=np.float32), (P, 1)),
    })
    c = [i["L0_attn_" + k].reshape(D) for k in
         ("ln1_w", "ln1_b", "ln2_w", "ln2_b", "time_decay", "time_first", "time_mix_k", "time_mix_v", "time_mix_r",
          "f_time_mix_k", "f_time_mix_r")]
    c += [i["L1_attn_bq"][by_q], i["L1_attn_bk"][by_k], np.tile(i["L1_attn_bk"], P // (KV * HD))]
    c += list(i["L0_ffn_b1"].reshape(FC, P))
    arrays["cols"] = np.ascontiguousarray(np.stack(c, axis=1))
    arrays["wqT"] = np.ascontiguousarray(i["L1_attn_Wq"][by_q].T)
    arrays["wq_n"] = np.ascontiguousarray(i["L1_attn_Wq"][by_q])
    arrays["wkT"] = np.ascontiguousarray(i["L1_attn_Wk"][by_k].T)
    arrays["wvT"] = np.ascontiguousarray(i["L1_attn_Wv"].T)
    arrays["woT"] = np.ascontiguousarray(i["L1_attn_Wo"].T)
    arrays["wexp"] = np.concatenate([
        i["L1_ffn_W1"], i["L1_ffn_b1"].reshape(EXPERTS, FC, P).transpose(0, 2, 1),
        i["L1_ffn_W2"].reshape(EXPERTS, FC, P, D).transpose(0, 2, 1, 3).reshape(EXPERTS, P, FC * D)],
        axis=2).reshape(EXPERTS * P, WROW)
    arrays["cT0"] = np.ascontiguousarray(i["L0_c"].T)
    arrays["cT1"] = np.ascontiguousarray(i["L1_c"].T)
    arrays["brow"] = np.concatenate([i["L1_attn_bo"], i["L0_ffn_b2"]])
    nc = _bacc.Bacc("TRN2", target_bir_lowering=False, num_devices=1)
    aps, feeds = {}, {}
    for name, v in arrays.items():
        feeds["in_" + name] = v
        aps[name] = nc.dram_tensor("in_" + name, v.shape, _mybir.dt.from_np(v.dtype), kind="ExternalInput").ap()
    aps["out"] = nc.dram_tensor("out_0_dram", (B * T, D), _mybir.dt.float32, kind="ExternalOutput").ap()
    program(nc, aps)
    r = _run(nc, [feeds], core_ids=[0])
    return r.results[0]["out_0_dram"].reshape(B, T, D)


_PLAIN = ["L0_attn_w_key", "L0_attn_w_value", "L0_attn_w_recept", "L0_attn_w_output", "L0_attn_f_w_key",
          "L0_attn_f_w_recept", "L0_attn_f_w_value", "L0_ffn_W1", "L0_ffn_W2", "L0_wmod", "L1_wmod", 
          "L1_attn_Wk", "L1_attn_bv", "L1_ffn_W_router", "L1_ffn_b_router", "L1_ffn_b2"]
```
